# Optimizing a Trainium2 kernel written in Bass

```python
import numpy as np
import jax
import jax.numpy as jnp

def _softmax(x, axis=-1):
    return jax.nn.softmax(x, axis=axis)

def _gelu(x):
    return jax.nn.gelu(x, approximate=True)

def _silu(x):
    return jax.nn.silu(x)

def _sigmoid(x):
    return jax.nn.sigmoid(x)

def _layernorm(x, axis=-1, eps=1e-05):
    m = jnp.mean(x, axis=axis, keepdims=True)
    v = jnp.var(x, axis=axis, keepdims=True)
    return (x - m) / jnp.sqrt(v + eps)

def _scatter_add(tgt, idx, src, axis=0):
    return tgt.at[idx].add(src)

def _segment_sum(src, seg, n):
    return jax.ops.segment_sum(src, seg, n)
kernel_name = 'mk_vit_tower_cls_d1_tok_img512_r4_7d6286'

def setup_inputs(seed: int=0):
    np.random.seed(seed)
    _w = jnp.asarray

    def _rec_inputs():
        import jax
        import jax.numpy as jnp
        _rk = jax.random.key(seed)
        x = -0.000121822 + 0.999869 * jax.random.normal(jax.random.fold_in(_rk, 1), (64, 3, 196, 196), jnp.float32)
        cls_tok = 0.02 * jax.random.normal(jax.random.fold_in(_rk, 5), (1, 1, 128), jnp.float32)
        return (x, cls_tok)
    x, cls_tok = _rec_inputs()

    def _L0_tok_setup():
        import jax, jax.numpy as jnp
        import numpy as np
        B, C, H, N_P, HID = (64, 3, 196, 14, 128)
        P = H // N_P
        IN_DIM = C * P * P
        SEQ = N_P * N_P + 1

        def sinusoidal_position(length, d):
            pos = jnp.arange(length, dtype=jnp.float32)[:, None]
            i = jnp.arange(d)[None, :]
            angle = pos / jnp.power(10000.0, (2 * (i // 2)).astype(jnp.float32) / d)
            return jnp.where(i % 2 == 0, jnp.sin(angle), jnp.cos(angle)).astype(jnp.float32)
        key = jax.random.key(seed)
        k_img, k_w, k_b, k_tok = jax.random.split(key, 4)
        img = jax.random.normal(k_img, (B, C, H, H), dtype=jnp.float32)
        W = jax.random.normal(k_w, (HID, IN_DIM), dtype=jnp.float32) / np.sqrt(IN_DIM)
        b = jax.random.normal(k_b, (HID,), dtype=jnp.float32) * 0.01
        token = jax.random.uniform(k_tok, (1, HID), dtype=jnp.float32)
        pos = sinusoidal_position(SEQ, HID)
        return {'img': img, 'W': W, 'b': b, 'token': token, 'pos': pos}
    _L0_tok_all = _L0_tok_setup()
    _L0_tok_in = {k: v for k, v in _L0_tok_all.items() if k in ('W', 'b', 'token', 'pos')}
    del _L0_tok_all

    def _L0_attn_setup():
        import math
        import jax, jax.numpy as jnp
        import numpy as np
        D_MODEL = 128
        N_HEADS = 8
        FACTOR = 5
        key = jax.random.key(seed)
        ks = jax.random.split(key, 9)
        B, L, d = (2, 512, D_MODEL)
        s = 0.02
        inp = {'x': jax.random.normal(ks[0], (B, L, d), dtype=jnp.float32)}
        inp['Wq'] = jax.random.normal(ks[1], (d, d), dtype=jnp.float32) * s
        inp['bq'] = jnp.zeros((d,), dtype=jnp.float32)
        inp['Wk'] = jax.random.normal(ks[2], (d, d), dtype=jnp.float32) * s
        inp['bk'] = jnp.zeros((d,), dtype=jnp.float32)
        inp['Wv'] = jax.random.normal(ks[3], (d, d), dtype=jnp.float32) * s
        inp['bv'] = jnp.zeros((d,), dtype=jnp.float32)
        inp['Wo'] = jax.random.normal(ks[4], (d, d), dtype=jnp.float32) * s
        inp['bo'] = jnp.zeros((d,), dtype=jnp.float32)
        return inp
    _L0_attn_all = _L0_attn_setup()
    _L0_attn_in = {k: v for k, v in _L0_attn_all.items() if k in ('Wq', 'bq', 'Wk', 'bk', 'Wv', 'bv', 'Wo', 'bo')}
    del _L0_attn_all

    def _L0_ffn_setup():
        import jax, jax.numpy as jnp
        import numpy as np
        B, S, D = (8, 2048, 128)
        E, DFF = (16, 128)
        CAPACITY = 2
        key = jax.random.key(seed)
        ks = jax.random.split(key, 4)
        x = jax.random.normal(ks[0], (B, S, D), dtype=jnp.float32)
        gate_weight = jax.random.normal(ks[1], (D, E), dtype=jnp.float32) * 0.006
        w1 = jax.random.normal(ks[2], (E, D, DFF), dtype=jnp.float32) * 0.02
        b1 = jnp.zeros((E, DFF), dtype=jnp.float32)
        w2 = jax.random.normal(ks[3], (E, DFF, D), dtype=jnp.float32) * 0.02
        b2 = jnp.zeros((E, D), dtype=jnp.float32)
        return {'x': x, 'gate_weight': gate_weight, 'w1': w1, 'b1': b1, 'w2': w2, 'b2': b2}
    _L0_ffn_all = _L0_ffn_setup()
    _L0_ffn_in = {k: v for k, v in _L0_ffn_all.items() if k in ('gate_weight', 'w1', 'b1', 'w2', 'b2')}
    del _L0_ffn_all
    return {'x': x, 'cls_tok': cls_tok, 'L0_tok_W': _L0_tok_in['W'], 'L0_tok_b': _L0_tok_in['b'], 'L0_tok_token': _L0_tok_in['token'], 'L0_tok_pos': _L0_tok_in['pos'], 'L0_attn_Wq': _L0_attn_in['Wq'], 'L0_attn_bq': _L0_attn_in['bq'], 'L0_attn_Wk': _L0_attn_in['Wk'], 'L0_attn_bk': _L0_attn_in['bk'], 'L0_attn_Wv': _L0_attn_in['Wv'], 'L0_attn_bv': _L0_attn_in['bv'], 'L0_attn_Wo': _L0_attn_in['Wo'], 'L0_attn_bo': _L0_attn_in['bo'], 'L0_ffn_gate_weight': _L0_ffn_in['gate_weight'], 'L0_ffn_w1': _L0_ffn_in['w1'], 'L0_ffn_b1': _L0_ffn_in['b1'], 'L0_ffn_w2': _L0_ffn_in['w2'], 'L0_ffn_b2': _L0_ffn_in['b2']}

def reference(x, cls_tok, L0_tok_W, L0_tok_b, L0_tok_token, L0_tok_pos, L0_attn_Wq, L0_attn_bq, L0_attn_Wk, L0_attn_bk, L0_attn_Wv, L0_attn_bv, L0_attn_Wo, L0_attn_bo, L0_ffn_gate_weight, L0_ffn_w1, L0_ffn_b1, L0_ffn_w2, L0_ffn_b2):
    import jax
    import jax.numpy as jnp

    def _L0_tok_ref(img, W, b, token, pos):
        import jax, jax.numpy as jnp
        import numpy as np
        B, C, H, N_P, HID = (64, 3, 196, 14, 128)
        P = H // N_P
        IN_DIM = C * P * P
        SEQ = N_P * N_P + 1

        def sinusoidal_position(length, d):
            pos = jnp.arange(length, dtype=jnp.float32)[:, None]
            i = jnp.arange(d)[None, :]
            angle = pos / jnp.power(10000.0, (2 * (i // 2)).astype(jnp.float32) / d)
            return jnp.where(i % 2 == 0, jnp.sin(angle), jnp.cos(angle)).astype(jnp.float32)
        Bn = img.shape[0]
        patches = img.reshape(Bn, C, N_P, P, N_P, P)
        patches = patches.transpose(0, 2, 4, 1, 3, 5).reshape(Bn, N_P * N_P, IN_DIM)
        tokens = jnp.einsum('bsd,hd->bsh', patches, W) + b
        cls = jnp.broadcast_to(token[None, :, :], (Bn, 1, HID))
        out = jnp.concatenate([cls, tokens], axis=1) + pos
        return out

    def _L0_attn_ref(x, Wq, bq, Wk, bk, Wv, bv, Wo, bo):
        import math
        import jax, jax.numpy as jnp
        import numpy as np
        D_MODEL = 128
        N_HEADS = 8
        FACTOR = 5
        B, L, d = x.shape
        H = N_HEADS
        E = d // H
        Q = (x @ Wq.T + bq).reshape(B, L, H, E).transpose(0, 2, 1, 3)
        K = (x @ Wk.T + bk).reshape(B, L, H, E).transpose(0, 2, 1, 3)
        V = (x @ Wv.T + bv).reshape(B, L, H, E).transpose(0, 2, 1, 3)
        scale = E ** 0.5
        attn = jnp.einsum('bhle,bhse->bhls', Q, K) / scale
        k = min(int(FACTOR * math.log(L)), L)
        topv, top_idx = jax.lax.top_k(attn, k)
        sm = jax.nn.softmax(topv, axis=-1)
        bi = jnp.arange(B)[:, None, None, None]
        hi = jnp.arange(H)[None, :, None, None]
        li = jnp.arange(L)[None, None, :, None]
        attn_w = jnp.zeros_like(attn).at[bi, hi, li, top_idx].set(sm)
        out = jnp.einsum('bhls,bhse->bhle', attn_w, V)
        out = out.transpose(0, 2, 1, 3).reshape(B, L, d)
        return out @ Wo.T + bo

    def _L0_ffn_ref(x, gate_weight, w1, b1, w2, b2):
        import jax, jax.numpy as jnp
        import numpy as np
        B, S, D = (8, 2048, 128)
        E, DFF = (16, 128)
        CAPACITY = 2
        Bx, Sx, Dx = x.shape
        num_experts = gate_weight.shape[1]
        k = Sx // num_experts * CAPACITY
        logits = jnp.einsum('bsd,de->bse', x, gate_weight)
        affinity = jax.nn.softmax(logits, axis=-1).transpose(0, 2, 1)
        gating, index = jax.lax.top_k(affinity, k)
        x_in = jnp.take_along_axis(x[:, None, :, :], index[..., None], axis=2)
        h = jax.nn.gelu(jnp.einsum('bekd,edh->bekh', x_in, w1) + b1[None, :, None, :])
        x_e = jnp.einsum('bekh,ehd->bekd', h, w2) + b2[None, :, None, :]
        weighted = gating[..., None] * x_e
        out = jnp.zeros_like(x)
        idx_flat = index.reshape(Bx, num_experts * k)
        vals_flat = weighted.reshape(Bx, num_experts * k, Dx)
        out = out.at[jnp.arange(Bx)[:, None], idx_flat].add(vals_flat)
        return out
    h = _L0_tok_ref(x, L0_tok_W, L0_tok_b, L0_tok_token, L0_tok_pos)
    h = jnp.concatenate([jnp.broadcast_to(cls_tok, (h.shape[0], 1, h.shape[2])), h], axis=1)
    h = h + _L0_attn_ref(_layernorm(h, axis=-1), L0_attn_Wq, L0_attn_bq, L0_attn_Wk, L0_attn_bk, L0_attn_Wv, L0_attn_bv, L0_attn_Wo, L0_attn_bo)
    h = h + _L0_ffn_ref(_layernorm(h, axis=-1), L0_ffn_gate_weight, L0_ffn_w1, L0_ffn_b1, L0_ffn_w2, L0_ffn_b2)
    return h

_drawn_inputs = setup_inputs


def setup_inputs(seed=0):
    import zlib

    import numpy as np

    out = dict(_drawn_inputs(seed))
    spreads = {'L0_attn_bq': (0.0, 0.8),
     'L0_attn_bk': (0.0, 0.8),
     'L0_attn_bv': (0.0, 0.465),
     'L0_attn_bo': (0.0, 0.1),
     'L0_ffn_b1': (0.0, 0.8),
     'L0_ffn_b2': (0.0, 0.8)}
    factors = {'cls_tok': 8.0,
     'L0_tok_b': 6.99,
     'L0_tok_token': 3.442,
     'L0_attn_Wq': 6.117,
     'L0_attn_Wk': 5.831,
     'L0_attn_Wv': 3.445,
     'L0_ffn_gate_weight': 7.298,
     'L0_ffn_w1': 8.0,
     'L0_ffn_w2': 8.0}
    for name, (base, spread) in spreads.items():
        noise = np.random.default_rng([zlib.crc32(name.encode()), seed]).standard_normal(out[name].shape)
        drawn = base * np.exp(spread * noise) if base else spread * noise
        out[name] = jnp.asarray(drawn.astype(out[name].dtype))
    for name, factor in factors.items():
        out[name] = (out[name] * factor).astype(out[name].dtype)
    return out
```

```python
import concourse.bass as bass
from concourse import mybir
from contextlib import ExitStack



def vit_block(nc, x, cls_tok, tok_W, tok_b, tok_token, tok_pos, Wq, bq, Wk, bk, Wv, bv, Wo, bo,
              gate_weight, w1, b1, w2, b2, out):
    f32 = mybir.dt.float32
    u32 = mybir.dt.uint32
    ALU = mybir.AluOpType
    ACT = mybir.ActivationFunctionType
    AX = mybir.AxisListType

    B, C, IMG, _ = x.shape
    D = tok_W.shape[0]
    P = 14
    NP = IMG // P
    L = NP * NP + 2
    LC = L // 2
    H = 8
    E = D // H
    NX = gate_weight.shape[1]
    KEEP = 26
    CAP = L // NX * 2
    SLOTS = NX * CAP
    EPC = 4
    NSC = NX // EPC
    SC = EPC * CAP
    G = 2
    NG = B // G
    R = G * 2
    SH = 3
    CP = C * P
    QS = -(-P // SH)
    XPAD = 2 * P
    NEG = -3.4028234663852886e38
    EPS = 1e-5

    TILES = []
    for i in range(G):
        TILES += [("full", i, h) for h in range(H)]
        TILES += [("half", i, h) for h in range(0, H, 2)]
    TILES += [("tail", 0, 0)]
    T = len(TILES)
    NT = T * NG
    TAILR = 64 // H
    NB = 5
    QPARTS = ((0, 128, 0), (H * 128, 64, 128), (H * 192, TAILR, L - TAILR))
    PE_LAG = 6
    EV_LAG = 5
    assert L == 198 and T == 25 and T % NB == 0 and G * H * TAILR == 128

    with ExitStack() as ctx:
        def sb(name, shape, dt=f32):
            return ctx.enter_context(nc.sbuf_tensor(name, shape, dt))

        def ps(name, shape):
            return ctx.enter_context(nc.psum_tensor(name, shape, f32))

        def sem(name):
            return ctx.enter_context(nc.semaphore(name))

        def sb2(name, shape, dt=f32):
            return [sb(f"{name}{p}", shape, dt) for p in range(2)]

        ident = sb("ident", [128, 128])
        ones_row = sb("ones_row", [1, LC])
        tokWT = sb("tokWT", [SH * CP, QS, D])
        posb = sb("posb", [LC, 2, D])
        eye_img = sb("eye_img", [G * NX, G])
        WT = sb("WT", [D, 4, D])
        bcol = sb("bcol", [D, 3])
        bq4 = sb("bq4", [D, 1])
        bo_row = sb("bo_row", [1, D])
        gw = sb("gw", [D, NX])
        w1s = sb("w1s", [D, NX, D])
        w2s = sb("w2s", [D, NX, D])
        b1s = sb("b1s", [NX, D])
        b2s = sb("b2s", [NX, D])
        img_sel = sb("img_sel", [G * NX, G, LC])
        own_exp = sb("own_exp", [G * NX, NX])
        slot_sel = sb("slot_sel", [CAP, EPC, SC])
        tok_iota = sb("tok_iota", [SC, L])
        tok_id = sb("tok_id", [LC, 2])
        eps_col = sb("eps_col", [LC, 1])

        X = sb("X", [SH * CP, G, XPAD + NP * IMG])
        Hs = sb("Hs", [LC, R, D])
        xn = sb("xn", [LC, R, D])
        xnT = sb("xnT", [D, G, L])
        QT = sb("QT", [D, G, L])
        QM = sb2("QM", [D, G, H * (128 + 64 + TAILR)])
        KT = sb2("KT", [D, G, L])
        V = sb2("V", [LC, R, D])
        VP = sb("VP", [LC, R, H, D])
        stats = sb("stats", [LC, R, 6])
        mv = sb("mv", [LC, R, 2])
        rstd = sb("rstd", [LC, 5, R])
        top = sb("top", [128, NB, 7 * 8])
        left = sb("left", [128, NB, L])
        ex = sb("ex", [128, NB, L])
        nmax = sb("nmax", [128, NB])
        extop = sb("extop", [128, KEEP])
        rsum = sb("rsum", [128, NB])
        rinv = sb("rinv", [128, NB])
        kept = sb("kept", [128, 2, L])
        prob = sb("prob", [128, 2, L])
        PT = [sb(f"PT{p}", [128, G, 2, H, L]) for p in range(2)]
        setup_room = PT[1][:, 0, :, :, :].rearrange("p c h l -> p (c h l)")
        wload = setup_room[:, 0:C * P * P]
        wraw = setup_room[:, 768:768 + 4 * D].rearrange("p (n d) -> p n d", n=4)
        wsort = setup_room[:, 1792:1792 + C * P * P]
        biasr = setup_room[0:LC, 1536:1536 + 2 * D].rearrange("p (c d) -> p c d", c=2)
        HR = sb2("HR", [LC, R, D])
        OT = sb("OT", [D, G, L])
        H1 = sb2("H1", [LC, R, D])
        xn2 = sb2("xn2", [LC, R, D])
        xn2T = sb("xn2T", [D, G, L])
        stats2 = sb("stats2", [LC, R, 6])
        mv2 = sb("mv2", [LC, R, 2])
        rstd2 = sb("rstd2", [LC, 5, R])
        lmax = sb("lmax", [LC, R])
        lsh = sb("lsh", [LC, R, NX])
        lex = sb("lex", [LC, R, NX])
        lsum = sb("lsum", [LC, R])
        linv = sb("linv", [LC, R])
        aff = sb("aff", [LC, 2, G, NX])
        affT = sb("affT", [G * NX, 3, L])
        route = sb("route", [G * NX, 2, CAP])
        idxu = sb("idxu", [G * NX, CAP], u32)
        routeT = sb("routeT", [CAP, 2, G, NSC, EPC])
        spread = sb("spread", [G * NX, NX, CAP])
        slotv = sb("slotv", [SC, 2, G, NSC])
        hotG = sb("hotG", [LC, R, SLOTS])
        hotS = sb("hotS", [SC, G, NSC, L])
        XG = sb("XG", [D, NX, G, CAP])
        HID = sb("HID", [D, NX, G * CAP])
        XE = XG[:, :, :, :].rearrange("p e i k -> p (e i k)").rearrange("p (i e k) -> p i e k", i=G, e=NX)
        XS = hotG[0:SC, :, :].rearrange("p r s -> p (r s)")[:, 0:G * NSC * D] \
            .rearrange("p (i c d) -> p i c d", i=G, c=NSC)
        Y = sb("Y", [LC, R, D])

        pS = [ps(f"pS{p}", [128, 512]) for p in range(2)]
        pT = [ps(f"pT{p}", [128, 512]) for p in range(2)]
        pO = ps("pO", [128, 512])
        pA = ps("pA", [128, 512])
        pD = [ps(f"pD{p}", [128, 512]) for p in range(2)]

        w_loaded = sem("w_loaded")
        ident_ready = sem("ident_ready")
        const_step = sem("const_step")
        zero_ready = sem("zero_ready")
        wsorted = sem("wsorted")
        wt_done = sem("wt_done")
        wt_copied = sem("wt_copied")
        posb_ready = sem("posb_ready")
        bq4_ready = sem("bq4_ready")
        x_loaded = sem("x_loaded")
        q_spread = [sem(f"q_spread{p}") for p in range(2)]
        hr_copied = sem("hr_copied")
        vp_made = sem("vp_made")
        stored = sem("stored")
        embedded = sem("embedded")
        h_copied = sem("h_copied")
        stat_step = sem("stat_step")
        var_exp = sem("var_exp")
        newton = sem("newton")
        xn_made = sem("xn_made")
        xnT_done = sem("xnT_done")
        xnT_copied = sem("xnT_copied")
        q_done = sem("q_done")
        q_copied = sem("q_copied")
        k_done = sem("k_done")
        k_copied = sem("k_copied")
        v_done = sem("v_done")
        v_copied = sem("v_copied")
        scored = sem("scored")
        top_found = [sem(f"top_found{r}") for r in range(4)]
        taken = [sem(f"taken{r}") for r in range(4)]
        nmax_made = sem("nmax_made")
        exp_made = sem("exp_made")
        sum_made = sem("sum_made")
        inv_made = sem("inv_made")
        kept_made = sem("kept_made")
        prob_made = sem("prob_made")
        pt_done = sem("pt_done")
        pt_copied = sem("pt_copied")
        pv_done = sem("pv_done")
        o_copied = sem("o_copied")
        proj_done = sem("proj_done")
        h1_copied = sem("h1_copied")
        stat2_step = sem("stat2_step")
        var2_exp = sem("var2_exp")
        newton2 = sem("newton2")
        xn2_made = sem("xn2_made")
        xn2T_done = sem("xn2T_done")
        xn2T_copied = sem("xn2T_copied")
        logit_done = sem("logit_done")
        lmax_made = sem("lmax_made")
        lsh_made = sem("lsh_made")
        lex_made = sem("lex_made")
        lsum_made = sem("lsum_made")
        linv_made = sem("linv_made")
        aff_made = sem("aff_made")
        affT_done = sem("affT_done")
        affT_copied = sem("affT_copied")
        route_step = sem("route_step")
        routed = sem("routed")
        routeT_done = sem("routeT_done")
        routeT_copied = sem("routeT_copied")
        spread_made = sem("spread_made")
        slot_done = sem("slot_done")
        slot_copied = sem("slot_copied")
        bc_done = sem("bc_done")
        hotG_made = sem("hotG_made")
        hotS_made = sem("hotS_made")
        xg_done = sem("xg_done")
        xg_copied = sem("xg_copied")
        m1_done = sem("m1_done")
        gelu_made = sem("gelu_made")
        m2_done = sem("m2_done")
        xe_copied = sem("xe_copied")
        xs_done = sem("xs_done")
        xs_copied = sem("xs_copied")
        y_done = sem("y_done")
        y_copied = sem("y_copied")

        N_W_LOADS = 20

        class Step:

            def __init__(self, half, par):
                self.half, self.par = half, par
                self.k = 2 * half + par

            def known(self):
                return isinstance(self.half, int)

            def runs(self, lag):
                return not self.known() or 0 <= self.k - lag < NG

            def group(self, lag):
                return self.k - lag

            def parity(self, lag):
                return (self.par - lag) % 2

            def rounds(self, lag):
                p = self.parity(lag)
                return self.half + (self.par - lag - p) // 2

            def tile(self, t):
                return Tile(self, t)

        class Tile:
            def __init__(self, step, t):
                back = t < 0
                self.n = (step.k - 1) * T + t
                self.valid = not step.known() or 0 <= self.n < NT
                self.par = ((step.par - 1) * T + t) % 2
                self.buf = t % NB
                self.gpar = step.parity(2 if back else 1)
                self.group = step.k - (2 if back else 1)
                self.t = t % T
                self.kind, self.img, self.head = TILES[self.t]

        def past(count):
            return max(count, 0) if isinstance(count, int) else count

        def settle(eng, *values):
            for v in values:
                if not isinstance(v, int):
                    eng.compute_val(v)
            eng.wait_ge(const_step, 1)

        def all_steps(body, eng):
            for k in range(4):
                body(Step(k // 2, k % 2))
            with eng.Fori(2, NG // 2 - 1) as half:
                body(Step(half, 0))
                body(Step(half, 1))
            for k in range(NG - 2, NG + 3):
                body(Step(k // 2, k % 2))

        block = ctx.enter_context(nc.Block())

        @block.sync
        def _(sp):
            def load_x(s):
                g = s.group(-1)
                sp.wait_ge(embedded, past(g))
                for i in range(G):
                    for sh in range(SH):
                        for c in range(C):
                            src = x[G * g + i, c].rearrange("(n p) w -> p n w", p=P)[:, :, sh:IMG] \
                                if s.known() else \
                                x[bass.ds(G * g + i, 1), c].rearrange("a (n p) w -> (a p) n w", p=P)[:, :, sh:IMG]
                            lo = (sh * C + c) * P
                            dst = X[lo:lo + P, i, XPAD:].rearrange("p (n w) -> p n w", n=NP)
                            sp.dma_start(dst[:, :, 0:IMG - sh], src).then_inc(x_loaded, 16)

            sp.wait_ge(zero_ready, 2)
            load_x(Step(-1, 1))
            sp.dma_start(wload[:, :], tok_W[:, :]).then_inc(w_loaded, 16)
            for n, w in enumerate((Wq, Wk, Wv, Wo)):
                sp.dma_start(wraw[:, n, :], w[:, :]).then_inc(w_loaded, 16)
            for n, v in enumerate((bq, bk, bv)):
                sp.dma_start(bcol[:, n:n + 1], v.rearrange("(p a) -> p a", a=1)).then_inc(w_loaded, 16)
            brow = tok_b.rearrange("(a n) -> a n", a=1)
            sp.dma_start(posb[1:LC, 0, :], tok_pos[0:LC - 1, :]).then_inc(w_loaded, 16)
            sp.dma_start(posb[:, 1, :], tok_pos[LC - 1:L - 1, :]).then_inc(w_loaded, 16)
            sp.dma_start(biasr[0:1, 0, :], cls_tok[0, :, :]).then_inc(w_loaded, 16)
            sp.dma_start(biasr[1:2, 0, :], tok_token[:, :]).then_inc(w_loaded, 16)
            sp.dma_start(biasr[2:LC, 0, :], brow.broadcast_to([LC - 2, D])).then_inc(w_loaded, 16)
            sp.dma_start(biasr[:, 1, :], brow.broadcast_to([LC, D])).then_inc(w_loaded, 16)
            sp.dma_start(bo_row[:, :], bo.rearrange("(a n) -> a n", a=1)).then_inc(w_loaded, 16)
            sp.dma_start(gw[:, :], gate_weight[:, :]).then_inc(w_loaded, 16)
            sp.dma_start(w1s[:, :, :], w1.rearrange("e d f -> d e f")).then_inc(w_loaded, 16)
            sp.dma_start(w2s[:, :, :], w2.rearrange("e f d -> f e d")).then_inc(w_loaded, 16)
            sp.dma_start(b1s[:, :], b1[:, :]).then_inc(w_loaded, 16)
            sp.dma_start(b2s[:, :], b2[:, :]).then_inc(w_loaded, 16)

            def body(s):
                if s.runs(1):
                    p = s.parity(1)
                    settle(sp, s.group(1) + 1, s.group(1) - 1)
                    sp.wait_ge(h_copied, s.group(1) + 1)
                    sp.wait_ge(proj_done, past(s.group(1) - 1))
                    sp.dma_start(HR[p][:, :, :], Hs[:, :, :]).then_inc(hr_copied, 16)
                if s.runs(-1):
                    load_x(s)
                if s.runs(0):
                    p = s.parity(0)
                    settle(sp, s.group(0) + 1, (s.group(0) - 1) * T)
                    sp.wait_ge(q_copied, s.group(0) + 1)
                    sp.wait_ge(scored, past((s.group(0) - 1) * T))
                    for h in range(H):
                        rows = slice(h * E, h * E + E)
                        for base, n, lo in QPARTS:
                            sp.dma_start(QM[p][rows, :, base + n * h:base + n * (h + 1)], QT[rows, :, lo:lo + n]) \
                              .then_inc(q_spread[p], 16)
                if s.runs(3):
                    g = s.group(3)
                    sp.wait_ge(y_copied, g + 1)
                    dst = out[G * g:G * g + G] if s.known() else out[bass.ds(G * g, G)]
                    sp.dma_start(dst.rearrange("b (c p) d -> p b c d", p=LC),
                                 Y[:, :, :].rearrange("p (b c) d -> p b c d", b=G)) \
                      .then_inc(stored, 16)

            all_steps(body, sp)
            sp.wait_ge(stored, 16 * NG)

        @block.gpsimd
        def _(pool):
            pool.memset(X[:, :, 0:XPAD], 0.0)
            pool.memset(ident[:, :], 0.0).then_inc(const_step, 1)
            pool.memset(posb[:, :, :], 0.0).then_inc(zero_ready, 2)
            pool.wait_ge(const_step, 1)
            pool.affine_select(out=ident[:, :], in_=ident[:, :], compare_op=ALU.not_equal, fill=1.0,
                               base=0, pattern=[[-1, 128]], channel_multiplier=1).then_inc(ident_ready, 1)
            pool.memset(VP[:, :, :, :], 0.0)
            for p in range(2):
                pool.memset(QM[p][:, :, :], 0.0).then_inc(zero_ready, 1)
            pool.memset(ones_row[:, :], 1.0)
            pool.memset(eps_col[:, :], EPS)
            pool.memset(img_sel[:, :, :], 1.0)
            pool.memset(own_exp[:, :], 0.0)
            pool.memset(slot_sel[:, :, :], 0.0)
            pool.memset(top[:, :, :], NEG)
            pool.iota(tok_iota[:, :], pattern=[[1, L]], base=0, channel_multiplier=0,
                      allow_small_or_imprecise_dtypes=True)
            pool.iota(tok_id[:, :], pattern=[[LC, 2]], base=0, channel_multiplier=1,
                      allow_small_or_imprecise_dtypes=True).then_inc(const_step, 1)
            pool.wait_ge(const_step, 2)
            for i in range(G):
                pool.affine_select(out=own_exp[:, :], in_=own_exp[:, :], compare_op=ALU.not_equal, fill=1.0,
                                   base=-NX * i, pattern=[[-1, NX]], channel_multiplier=1) \
                    .then_inc(const_step, 1)
                pool.wait_ge(const_step, 3 + i)
            pool.affine_select(out=slot_sel[:, :, :], in_=slot_sel[:, :, :], compare_op=ALU.not_equal, fill=1.0,
                               base=0, pattern=[[CAP, EPC], [-1, SC]], channel_multiplier=1)
            pool.affine_select(out=img_sel[:, :, :], in_=img_sel[:, :, :], compare_op=ALU.is_ge, fill=0.0,
                               base=0, pattern=[[-NX, G], [0, LC]], channel_multiplier=1) \
                .then_inc(const_step, 1)
            pool.wait_ge(const_step, 3 + G)
            pool.affine_select(out=img_sel[:, :, :], in_=img_sel[:, :, :], compare_op=ALU.is_ge, fill=0.0,
                               base=NX - 1, pattern=[[NX, G], [0, LC]], channel_multiplier=-1) \
                .then_inc(const_step, 1)

            def refine(mvt, r, exped, done, n):
                var = mvt[:, :, 1]
                settle(pool, 2 * n + 2)
                pool.wait_ge(exped, 2 * n + 2)
                pool.tensor_tensor(r[:, 4, :], r[:, 1, :], r[:, 1, :], ALU.mult).then_inc(done, 1)
                pool.tensor_scalar(r[:, 0, :], var, EPS, -0.5, ALU.add, ALU.mult).then_inc(done, 1)
                pool.wait_ge(done, 7 * n + 2)
                pool.tensor_tensor(r[:, 4, :], r[:, 4, :], r[:, 0, :], ALU.mult).then_inc(done, 1)
                settle(pool, 7 * n + 3)
                pool.wait_ge(done, 7 * n + 3)
                pool.tensor_scalar(r[:, 4, :], r[:, 4, :], 1.5, None, ALU.add).then_inc(done, 1)
                pool.wait_ge(done, 7 * n + 4)
                pool.tensor_tensor(r[:, 2, :], r[:, 4, :], r[:, 1, :], ALU.mult).then_inc(done, 1)
                pool.wait_ge(done, 7 * n + 5)
                pool.tensor_tensor(r[:, 3, :], mvt[:, :, 0], r[:, 2, :], ALU.mult).then_inc(done, 1)
                settle(pool, 7 * n + 6)
                pool.wait_ge(done, 7 * n + 6)
                pool.tensor_scalar(r[:, 3, :], r[:, 3, :], -1.0, None, ALU.mult).then_inc(done, 1)

            def body(s):
                for t in range(T):
                    if t == 5 and s.runs(0):
                        refine(mv, rstd, var_exp, newton, s.group(0))
                    if t == 16 and s.runs(2):
                        refine(mv2, rstd2, var2_exp, newton2, s.group(2))
                    if t == 3 and s.runs(2):
                        g = s.group(2)
                        settle(pool, g + 1)
                        pool.wait_ge(v_copied, g + 1)
                        pool.wait_ge(pv_done, past(g))
                        flat = VP[:, :, :, :].rearrange("p r h d -> p r (h d)")
                        dst = bass.AP(tensor=flat.tensor, offset=flat.offset,
                                      ap=[list(flat.ap[0]), [H * D, R], [D + E, H], [1, E]])
                        pool.tensor_copy(dst, V[s.parity(2)][:, :, :].rearrange("p r (h e) -> p r h e", h=H)) \
                            .then_inc(vp_made, 1)
                    if t == 0 and s.runs(3):
                        g = s.group(3)
                        pool.wait_ge(linv_made, g + 1)
                        pool.wait_ge(affT_done, past(g))
                        pool.tensor_tensor(aff[:, :, :, :].rearrange("p c i e -> p i c e"),
                                           lex[:, :, :].rearrange("p (i c) e -> p i c e", i=G),
                                           linv[:, :].rearrange("p (i c a) -> p i c a", i=G, a=1)
                                           .broadcast_to([LC, G, 2, NX]), ALU.mult).then_inc(aff_made, 1)
                    if t == 6 and s.runs(3):
                        g = s.group(3)
                        pool.wait_ge(routed, g + 1)
                        pool.wait_ge(bc_done, past(G * g))
                        pool.tensor_tensor(spread[:, :, :],
                                           route[:, 0:1, :].broadcast_to([G * NX, NX, CAP]),
                                           own_exp[:, :].rearrange("p (e a) -> p e a", a=1)
                                           .broadcast_to([G * NX, NX, CAP]), ALU.mult).then_inc(spread_made, 1)
                    q = s.tile(t - 2)
                    if q.valid:
                        settle(pool, q.n + 1, q.n - 1)
                        pool.wait_ge(inv_made, q.n + 1)
                        pool.wait_ge(taken[3], q.n + 1)
                        pool.wait_ge(prob_made, past(q.n - 1))
                        pool.tensor_scalar(kept[:, q.par, :], left[:, q.buf, :], NEG, rinv[:, q.buf:q.buf + 1],
                                           ALU.is_equal, ALU.mult).then_inc(kept_made, 1)
                        pool.wait_ge(kept_made, q.n + 1)
                        pool.wait_ge(exp_made, q.n + 1)
                        pool.wait_ge(pt_done, past(q.n - 1))
                        pool.tensor_tensor(prob[:, q.par, :], kept[:, q.par, :], ex[:, q.buf, :], ALU.mult) \
                            .then_inc(prob_made, 1)

            all_steps(body, pool)

        @block.vector
        def _(dve):
            dve.wait_ge(w_loaded, 16 * N_W_LOADS)
            dve.wait_ge(zero_ready, 2)
            dve.tensor_tensor(posb[:, :, :], posb[:, :, :], biasr[:, :, :], ALU.add).then_inc(posb_ready, 1)
            dve.wait_ge(const_step, 4 + G)

            def found(q, r):
                settle(dve, q.n + 1, q.n - NB + 1)
                if r == 0:
                    dve.wait_ge(scored, q.n + 1)
                    dve.wait_ge(inv_made, past(q.n - NB + 1))
                else:
                    dve.wait_ge(taken[r - 1], q.n + 1)
                src = pS[q.par][:, 0:L] if r == 0 else left[:, q.buf, :]
                dve.max(top[:, q.buf, 8 * r:8 * r + 8], src).then_inc(top_found[r], 1)

            def take(q, r):
                settle(dve, q.n + 1, q.n - NB + 1)
                dve.wait_ge(top_found[r], q.n + 1)
                if r == 0:
                    dve.wait_ge(kept_made, past(q.n - NB + 1))
                src = pS[q.par][:, 0:L] if r == 0 else left[:, q.buf, :]
                what = top[:, q.buf, 8 * r:8 * r + 8]
                if r == 3:
                    what = top[:, q.buf, 24:56].rearrange("p (a b) -> p a b", b=8)[:, :, 0:2]
                dve.match_replace(left[:, q.buf, :], what, src, NEG).then_inc(taken[r], 1)

            def layer_stats(src, ready, st, mvt, step, refined, n):
                dve.wait_ge(ready, n + 1)
                dve.wait_ge(refined, past(7 * n))
                for r in range(R):
                    dve.bn_stats(st[:, r, :], src[:, r, :]).then_inc(step, 1)
                settle(dve, 2 * R * n + R)
                dve.wait_ge(step, 2 * R * n + R)
                for r in range(R):
                    dve.bn_aggr(mvt[:, r, :], st[:, r, :]).then_inc(step, 1)

            def body(s):
                for t in range(T):
                    q, o, f = s.tile(t), s.tile(t - 1), s.tile(t - 2)
                    if q.valid:
                        found(q, 0)
                    if o.valid:
                        found(o, 2)
                    if q.valid:
                        take(q, 0)
                    if o.valid:
                        take(o, 2)
                    if q.valid:
                        dve.wait_ge(exp_made, past(q.n - NB + 1))
                        dve.tensor_scalar(nmax[:, q.buf:q.buf + 1], top[:, q.buf, 0:1], -1.0, None, ALU.mult) \
                           .then_inc(nmax_made, 1)
                    if o.valid:
                        found(o, 3)
                    if q.valid:
                        found(q, 1)
                    if o.valid:
                        take(o, 3)
                    if q.valid:
                        take(q, 1)
                    if f.valid:
                        dve.wait_ge(sum_made, f.n + 1)
                        dve.wait_ge(kept_made, past(f.n - NB + 1))
                        dve.reciprocal(rinv[:, f.buf:f.buf + 1], rsum[:, f.buf:f.buf + 1]).then_inc(inv_made, 1)

                    if t == 5 and s.runs(0):
                        layer_stats(Hs, h_copied, stats, mv, stat_step, newton, s.group(0))
                    if t == 16 and s.runs(2):
                        layer_stats(H1[s.parity(2)], h1_copied, stats2, mv2, stat2_step, newton2, s.group(2))
                    if t == 22 and s.runs(2):
                        g = s.group(2)
                        lg = pA[0:LC, 0:R * NX].rearrange("p (r e) -> p r e", r=R)
                        dve.wait_ge(logit_done, g + 1)
                        dve.tensor_reduce(lmax[:, :], lg, axis=AX.X, op=ALU.max).then_inc(lmax_made, 1)
                        dve.wait_ge(lmax_made, g + 1)
                        dve.wait_ge(lex_made, past(g))
                        dve.tensor_tensor(lsh[:, :, :], lg, lmax[:, :].rearrange("p (r a) -> p r a", a=1)
                                          .broadcast_to([LC, R, NX]), ALU.subtract).then_inc(lsh_made, 1)
                    if t == 24 and s.runs(2):
                        g = s.group(2)
                        dve.wait_ge(lex_made, g + 1)
                        dve.tensor_reduce(lsum[:, :], lex[:, :, :], axis=AX.X, op=ALU.add).then_inc(lsum_made, 1)
                        dve.wait_ge(lsum_made, g + 1)
                        dve.wait_ge(aff_made, past(g))
                        dve.reciprocal(linv[:, :], lsum[:, :]).then_inc(linv_made, 1)
                    if t in (4, 5, 6) and s.runs(3):
                        g, r = s.group(3), t - 4
                        n = 8 * g + 3 * r
                        a = affT[:, r, :]
                        settle(dve, g + 1, g, n)
                        if r == 0:
                            dve.wait_ge(affT_copied, g + 1)
                            dve.wait_ge(spread_made, past(g))
                            dve.wait_ge(routeT_done, past(g))
                        else:
                            dve.wait_ge(route_step, past(n))
                        m = route[:, 1, 8 * r:8 * r + 8]
                        dve.max(m, a).then_inc(route_step, 1)
                        settle(dve, n + 1)
                        dve.wait_ge(route_step, n + 1)
                        dve.max_index(idxu[:, 8 * r:8 * r + 8], m, a).then_inc(route_step, 1)
                        if r < 2:
                            dve.match_replace(affT[:, r + 1, :], m, a, NEG).then_inc(route_step, 1)
                        else:
                            dve.wait_ge(route_step, n + 2)
                            dve.tensor_copy(route[:, 0, :], idxu[:, :]).then_inc(routed, 1)
                    if t in (10, 11) and s.runs(3):
                        i, g = t - 10, s.group(3)
                        dve.wait_ge(bc_done, G * g + i + 1)
                        dve.wait_ge(y_done, past(g))
                        for c in range(2):
                            dve.tensor_scalar(hotG[:, 2 * i + c, :], pD[i][0:LC, 0:SLOTS], tok_id[:, c:c + 1], None,
                                              ALU.is_equal).then_inc(hotG_made, 1)
                    if t in (12, 13) and s.runs(3):
                        i, g = t - 12, s.group(3)
                        dve.wait_ge(slot_copied, g + 1)
                        dve.wait_ge(y_done, past(g))
                        for c in range(NSC):
                            dve.tensor_scalar(hotS[:, i, c, :], tok_iota[:, :], slotv[:, 0, i, c:c + 1],
                                              slotv[:, 1, i, c:c + 1], ALU.is_equal, ALU.mult).then_inc(hotS_made, 1)

            all_steps(body, dve)

        @block.scalar
        def _(act):
            act.wait_ge(w_loaded, 16 * N_W_LOADS)
            act.activation(wsort.rearrange("d (q c) -> d q c", q=P), wload.rearrange("d (c q) -> d q c", q=P),
                           ACT.Copy).then_inc(wsorted, 1)
            for n in range(QS + 4):
                act.wait_ge(wt_done, n + 1)
                if n < QS:
                    rows = min(SH, P - SH * n) * CP
                    act.activation(tokWT[0:rows, n, :], pT[n % 2][0:rows, 0:D], ACT.Copy).then_inc(wt_copied, 1)
                else:
                    act.activation(WT[:, n - QS, :], pT[n % 2][:, 0:D], ACT.Copy).then_inc(wt_copied, 1)
            act.activation(bq4[:, :], bcol[:, 0:1], ACT.Copy, scale=0.25).then_inc(bq4_ready, 1)
            act.wait_ge(bq4_ready, 1)

            def inv_std(mvt, r, step, exped, refined, n):
                act.wait_ge(step, past(2 * R * n + 2 * R))
                act.wait_ge(refined, past(7 * n))
                act.activation(r[:, 0, :], mvt[:, :, 1], ACT.Ln, bias=eps_col[:, 0:1]).then_inc(exped, 1)
                act.wait_ge(exped, 2 * n + 1)
                act.activation(r[:, 1, :], r[:, 0, :], ACT.Exp, scale=-0.5).then_inc(exped, 1)

            def body(s):
                for t in range(T):
                    q, o, m = s.tile(t), s.tile(t - 1), s.tile(t - EV_LAG)
                    if q.valid:
                        act.wait_ge(nmax_made, q.n + 1)
                        act.wait_ge(taken[0], q.n + 1)
                        act.wait_ge(prob_made, past(q.n - NB + 1))
                        act.activation(ex[:, q.buf, :], pS[q.par][:, 0:L], ACT.Exp, bias=nmax[:, q.buf:q.buf + 1]) \
                           .then_inc(exp_made, 1)
                    if o.valid:
                        act.wait_ge(top_found[3], o.n + 1)
                        act.wait_ge(inv_made, past(o.n - NB + 1))
                        act.wait_ge(sum_made, past(o.n))
                        act.activation(extop[:, :], top[:, o.buf, 0:KEEP], ACT.Exp, bias=nmax[:, o.buf:o.buf + 1],
                                       accum_out=rsum[:, o.buf:o.buf + 1]).then_inc(sum_made, 1)
                    if m.valid:
                        act.wait_ge(pt_done, m.n + 1)
                        if m.t == 0:
                            act.wait_ge(pv_done, past(m.group - 1))
                        dst, src = PT[m.gpar][0:LC], pT[m.par][0:LC, 0:256].rearrange("p (c r) -> p c r", c=2)
                        if m.kind == "full":
                            act.activation(dst[:, m.img, :, m.head, 0:128], src, ACT.Copy).then_inc(pt_copied, 1)
                        elif m.kind == "half":
                            act.activation(dst[:, m.img, :, m.head:m.head + 2, 128:192],
                                           src.rearrange("p c (h r) -> p c h r", h=2), ACT.Copy) \
                               .then_inc(pt_copied, 1)
                        else:
                            for i in range(G):
                                v = src[:, :, 64 * i:64 * i + 64].rearrange("p c (h r) -> p c h r", h=H)
                                ins = act.activation(dst[:, i, :, :, 192:L], v[:, :, :, TAILR - (L - 192):TAILR],
                                                     ACT.Copy)
                            ins.then_inc(pt_copied, 1)

                    if t == 3 and s.runs(3):
                        g = s.group(3)
                        act.wait_ge(affT_done, g + 1)
                        act.wait_ge(route_step, past(8 * g))
                        act.activation(affT[:, 0, :], pD[0][0:G * NX, 0:L], ACT.Copy).then_inc(affT_copied, 1)
                    if t == 4 and s.runs(0):
                        g = s.group(0)
                        act.wait_ge(embedded, g + 1)
                        act.wait_ge(hr_copied, past(16 * g))
                        act.activation(Hs[:, :, :], pA[0:LC, 0:R * D].rearrange("p (r d) -> p r d", r=R), ACT.Copy) \
                           .then_inc(h_copied, 1)
                    if t == 6 and s.runs(0):
                        inv_std(mv, rstd, stat_step, var_exp, newton, s.group(0))
                    if t == 8 and s.runs(0):
                        g = s.group(0)
                        act.wait_ge(newton, 7 * g + 7)
                        act.wait_ge(xnT_done, past(g))
                        for r in range(R):
                            act.activation(xn[:, r, :], Hs[:, r, :], ACT.Identity,
                                           bias=rstd[:, 3, r:r + 1], scale=rstd[:, 2, r:r + 1]).then_inc(xn_made, 1)
                    if t == 8 and s.runs(3):
                        g = s.group(3)
                        act.wait_ge(routeT_done, g + 1)
                        act.wait_ge(slot_done, past(g))
                        act.activation(routeT[:, :, :, :, :],
                                       pD[0][0:CAP, 0:2 * G * NX].rearrange("p (v i c j) -> p v i c j", v=2, i=G, c=NSC),
                                       ACT.Copy).then_inc(routeT_copied, 1)
                    if t == 9 and s.runs(3):
                        g = s.group(3)
                        act.wait_ge(slot_done, g + 1)
                        act.wait_ge(hotS_made, past(G * NSC * g))
                        act.activation(slotv[:, :, :, :],
                                       pD[1][0:SC, 0:2 * G * NSC].rearrange("p (v i c) -> p v i c", v=2, i=G),
                                       ACT.Copy).then_inc(slot_copied, 1)
                    if t == 10 and s.runs(0):
                        g = s.group(0)
                        act.wait_ge(xnT_done, g + 1)
                        act.wait_ge(v_done, past(g))
                        act.activation(xnT[:, :, :], pA[:, 0:G * L].rearrange("p (i l) -> p i l", i=G), ACT.Copy) \
                           .then_inc(xnT_copied, 1)
                    if t == 11 and s.runs(0):
                        p, g = s.parity(-1), s.group(0)
                        act.wait_ge(q_done, g + 1)
                        act.wait_ge(q_spread[p], past(16 * 3 * H * s.rounds(-1)))
                        act.activation(QT[:, :, :], pA[:, 0:G * L].rearrange("p (i l) -> p i l", i=G), ACT.Identity,
                                       bias=bq4[:, 0:1], scale=0.25).then_inc(q_copied, 1)
                    if t == 13 and s.runs(0):
                        p, g = s.parity(0), s.group(0)
                        act.wait_ge(k_done, g + 1)
                        act.activation(KT[p][:, :, :], pA[:, 0:G * L].rearrange("p (i l) -> p i l", i=G), ACT.Identity,
                                       bias=bcol[:, 1:2]).then_inc(k_copied, 1)
                    if t == 15 and s.runs(0):
                        p, g = s.parity(0), s.group(0)
                        act.wait_ge(v_done, g + 1)
                        act.wait_ge(vp_made, past(g - 1))
                        act.activation(V[p][:, :, :], pA[0:LC, 0:R * D].rearrange("p (r d) -> p r d", r=R), ACT.Copy) \
                           .then_inc(v_copied, 1)
                    if t in (12, 13) and s.runs(3):
                        g, i = s.group(3), t - 12
                        act.wait_ge(xg_done, G * g + i + 1)
                        act.wait_ge(xs_done, past(G * g))
                        act.activation(XG[:, :, i, :], pD[i][:, 0:SLOTS].rearrange("p (e k) -> p e k", e=NX), ACT.Copy) \
                           .then_inc(xg_copied, 1)
                    if t == 13 and s.runs(2):
                        g = s.group(2)
                        act.wait_ge(pv_done, g + 1)
                        act.wait_ge(proj_done, past(g))
                        act.activation(OT[:, :, :], pO[:, 0:G * L].rearrange("p (i l) -> p i l", i=G), ACT.Identity,
                                       bias=bcol[:, 2:3]).then_inc(o_copied, 1)
                    if t == 16 and s.runs(2):
                        p, g = s.parity(2), s.group(2)
                        act.wait_ge(proj_done, g + 1)
                        act.wait_ge(y_done, past(g - 1))
                        act.activation(H1[p][:, :, :], pO[0:LC, 0:R * D].rearrange("p (r d) -> p r d", r=R), ACT.Copy) \
                           .then_inc(h1_copied, 1)
                    if t == 16 and s.runs(3):
                        g = s.group(3)
                        for a in range(2):
                            act.wait_ge(m1_done, 2 * g + a + 1)
                            act.wait_ge(m2_done, past(2 * g))
                            act.activation(HID[:, NX // 2 * a:NX // 2 * (a + 1), :],
                                           pD[a][:, 0:SLOTS].rearrange("p (e k) -> p e k", e=NX // 2),
                                           ACT.Gelu_apprx_tanh).then_inc(gelu_made, 1)
                    if t == 17 and s.runs(2):
                        inv_std(mv2, rstd2, stat2_step, var2_exp, newton2, s.group(2))
                    if t == 18 and s.runs(3):
                        g = s.group(3)
                        for a in range(2):
                            act.wait_ge(m2_done, 2 * g + a + 1)
                            act.wait_ge(xs_done, past(G * g))
                            act.activation(XE[:, :, NX // 2 * a:NX // 2 * (a + 1), :].rearrange("p i e k -> p e i k"),
                                           pD[a][:, 0:SLOTS].rearrange("p (e i k) -> p e i k", e=NX // 2, i=G),
                                           ACT.Copy).then_inc(xe_copied, 1)
                    if t == 19 and s.runs(2):
                        p, g = s.parity(2), s.group(2)
                        act.wait_ge(newton2, 7 * g + 7)
                        act.wait_ge(xg_done, past(G * (g - 1)))
                        for r in range(R):
                            act.activation(xn2[p][:, r, :], H1[p][:, r, :], ACT.Identity,
                                           bias=rstd2[:, 3, r:r + 1], scale=rstd2[:, 2, r:r + 1]).then_inc(xn2_made, 1)
                    if t == 20 and s.runs(3):
                        g = s.group(3)
                        for i in range(G):
                            act.wait_ge(xs_done, G * g + i + 1)
                            act.wait_ge(y_done, past(g))
                            act.activation(XS[:, i, :, :], pD[i][0:SC, 0:NSC * D].rearrange("p (c d) -> p c d", c=NSC),
                                           ACT.Copy).then_inc(xs_copied, 1)
                    if t == 21 and s.runs(2):
                        g = s.group(2)
                        act.wait_ge(xn2T_done, g + 1)
                        act.wait_ge(logit_done, past(g))
                        act.activation(xn2T[:, :, :], pA[:, 0:G * L].rearrange("p (i l) -> p i l", i=G), ACT.Copy) \
                           .then_inc(xn2T_copied, 1)
                    if t == 23 and s.runs(2):
                        g = s.group(2)
                        act.wait_ge(lsh_made, g + 1)
                        act.wait_ge(aff_made, past(g))
                        act.activation(lex[:, :, :], lsh[:, :, :], ACT.Exp).then_inc(lex_made, 1)
                    if t == 24 and s.runs(3):
                        g = s.group(3)
                        act.wait_ge(y_done, g + 1)
                        act.wait_ge(stored, past(16 * g))
                        act.activation(Y[:, :, :], pD[0][0:LC, 0:R * D].rearrange("p (r d) -> p r d", r=R), ACT.Copy) \
                           .then_inc(y_copied, 1)

            all_steps(body, act)

        @block.tensor
        def _(pe):
            pe.wait_ge(w_loaded, 16 * N_W_LOADS)
            pe.wait_ge(ident_ready, 1)
            pe.wait_ge(wsorted, 1)
            for n in range(QS + 4):
                pe.wait_ge(wt_copied, past(n - 1))
                if n < QS:
                    cols = min(SH, P - SH * n)
                    src = wsort[:, SH * n * CP:(SH * n + cols) * CP]
                    pe.transpose(pT[n % 2][0:cols * CP, 0:D], src, ident[:, :]).then_inc(wt_done, 1)
                else:
                    pe.transpose(pT[n % 2][:, 0:D], wraw[:, n - QS, :], ident[:, :]).then_inc(wt_done, 1)
            pe.wait_ge(wt_copied, QS + 4)
            pe.wait_ge(posb_ready, 1)
            pe.wait_ge(const_step, 4 + G)
            pe.wait_ge(zero_ready, 4)

            def chunk(i, c):
                return slice(i * L + c * LC, i * L + (c + 1) * LC)

            def score(q, par):
                pe.wait_ge(exp_made, past(q.n - 1))
                if q.t == 0:
                    pe.wait_ge(k_copied, q.group + 1)
                qm, k = QM[q.gpar], KT[q.gpar]
                dst = pS[q.par]
                if q.kind == "full":
                    pe.matmul(dst[:, 0:L], qm[:, q.img, 128 * q.head:128 * q.head + 128], k[:, q.img, :], start=True, stop=True) \
                      .then_inc(scored, 1)
                elif q.kind == "half":
                    lo = QPARTS[1][0] + 64 * q.head
                    pe.matmul(dst[:, 0:L], qm[:, q.img, lo:lo + 128], k[:, q.img, :],
                              start=True, stop=True).then_inc(scored, 1)
                else:
                    for i in range(G):
                        ins = pe.matmul(dst[64 * i:64 * i + 64, 0:L], qm[:, i, QPARTS[2][0]:], k[:, i, :],
                                        start=True, stop=True)
                    ins.then_inc(scored, 1)

            def body(s):
                for t in range(T):
                    q, m = s.tile(t), s.tile(t - PE_LAG)
                    if q.valid:
                        if t == 0:
                            pe.wait_ge(q_spread[q.gpar], 16 * 3 * H * (s.rounds(1) + 1))
                        score(q, s.par)

                    if t < 6 and s.runs(0):
                        g = s.group(0)
                        if t == 0:
                            pe.wait_ge(x_loaded, 16 * G * SH * C * (g + 1))
                            pe.wait_ge(v_copied, past(g))
                            pe.wait_ge(lsh_made, past(g - 2))
                        for n in range(4 * t, 4 * t + 4):
                            r, part = divmod(n, QS + 1)
                            i, c = divmod(r, 2)
                            dst = pA[0:LC, r * D:r * D + D]
                            if part < QS:
                                kp = min(SH, P - SH * part) * CP
                                lo = XPAD + P * (LC * c - 2) + SH * part
                                src = X[0:kp, i, lo:lo + P * (LC - 1) + 1:P]
                                ins = pe.matmul(dst, src, tokWT[0:kp, part, :], start=part == 0, stop=False)
                            else:
                                ins = pe.matmul(dst, ident[0:LC, 0:LC], posb[:, c, :], start=False, stop=True)
                        if t == 5:
                            ins.then_inc(embedded, 1)
                    if t == 11 and s.runs(0):
                        g = s.group(0)
                        pe.wait_ge(xn_made, R * g + R)
                        for r in range(R):
                            ins = pe.transpose(pA[:, chunk(r // 2, r % 2)], xn[:, r, :], ident[0:LC, 0:LC])
                        ins.then_inc(xnT_done, 1)
                    if t == 12 and s.runs(0):
                        pe.wait_ge(xnT_copied, s.group(0) + 1)
                        pe.matmul(pA[:, 0:G * L], WT[:, 0, :], xnT[:, :, :], start=True, stop=True).then_inc(q_done, 1)
                    if t == 14 and s.runs(0):
                        pe.wait_ge(q_copied, s.group(0) + 1)
                        pe.matmul(pA[:, 0:G * L], WT[:, 1, :], xnT[:, :, :], start=True, stop=True).then_inc(k_done, 1)
                    if t == 16 and s.runs(0):
                        pe.wait_ge(k_copied, s.group(0) + 1)
                        for r in range(R):
                            ins = pe.matmul(pA[0:LC, r * D:r * D + D], xnT[:, r // 2, LC * (r % 2):LC * (r % 2 + 1)],
                                            WT[:, 2, :], start=True, stop=True)
                        ins.then_inc(v_done, 1)

                    if 6 <= t < 14 and s.runs(2):
                        p, g = s.parity(2), s.group(2)
                        if t == 6:
                            pe.wait_ge(pt_copied, (g + 1) * T)
                            pe.wait_ge(vp_made, g + 1)
                            pe.wait_ge(h1_copied, past(g))
                        for n in range(4 * (t - 6), 4 * (t - 6) + 4):
                            i, h, c = n // (2 * H), n // 2 % H, n % 2
                            ins = pe.matmul(pO[:, i * L:i * L + L], VP[:, 2 * i + c, h, :], PT[p][0:LC, i, c, h, :],
                                            start=n % (2 * H) == 0, stop=n % (2 * H) == 2 * H - 1)
                        if t == 13:
                            ins.then_inc(pv_done, 1)
                    if t in (15, 16) and s.runs(2):
                        p, g = s.parity(2), s.group(2)
                        if t == 15:
                            pe.wait_ge(o_copied, g + 1)
                            pe.wait_ge(hr_copied, 16 * (g + 1))
                        for r in range(2 * (t - 15), 2 * (t - 15) + 2):
                            dst = pO[0:LC, r * D:r * D + D]
                            pe.matmul(dst, OT[:, r // 2, LC * (r % 2):LC * (r % 2 + 1)], WT[:, 3, :],
                                      start=True, stop=False)
                            pe.matmul(dst, ident[0:LC, 0:LC], HR[p][:, r, :], start=False, stop=False)
                            ins = pe.matmul(dst, ones_row[:, :], bo_row[:, :], start=False, stop=True)
                        if t == 16:
                            ins.then_inc(proj_done, 1)
                    if t == 21 and s.runs(2):
                        g = s.group(2)
                        pe.wait_ge(xn2_made, R * g + R)
                        if s.runs(0):
                            pe.wait_ge(v_copied, s.group(0) + 1)
                        for r in range(R):
                            ins = pe.transpose(pA[:, chunk(r // 2, r % 2)], xn2[s.parity(2)][:, r, :],
                                               ident[0:LC, 0:LC])
                        ins.then_inc(xn2T_done, 1)
                    if t == 23 and s.runs(2):
                        g = s.group(2)
                        pe.wait_ge(xn2T_copied, g + 1)
                        for r in range(R):
                            ins = pe.matmul(pA[0:LC, r * NX:r * NX + NX],
                                            xn2T[:, r // 2, LC * (r % 2):LC * (r % 2 + 1)], gw[:, :],
                                            start=True, stop=True)
                        ins.then_inc(logit_done, 1)

                    if t == 4 and s.runs(3):
                        g = s.group(3)
                        pe.wait_ge(aff_made, g + 1)
                        pe.wait_ge(y_copied, past(g))
                        for c in range(2):
                            ins = pe.transpose(pD[0][0:G * NX, LC * c:LC * c + LC],
                                               aff[:, c, :, :].rearrange("p i e -> p (i e)"), ident[0:LC, 0:LC])
                        ins.then_inc(affT_done, 1)
                    if t == 9 and s.runs(3):
                        g = s.group(3)
                        settle(pe, g + 1)
                        pe.wait_ge(routed, g + 1)
                        for v in range(2):
                            ins = pe.transpose(pD[0][0:CAP, G * NX * v:G * NX * (v + 1)], route[:, v, :],
                                               ident[0:G * NX, 0:G * NX])
                        ins.then_inc(routeT_done, 1)
                    if t == 10 and s.runs(3):
                        g = s.group(3)
                        pe.wait_ge(routeT_copied, g + 1)
                        for j in range(EPC):
                            ins = pe.matmul(pD[1][0:SC, 0:2 * G * NSC], slot_sel[:, j, :],
                                            routeT[:, :, :, :, j].rearrange("p v i c -> p (v i c)"),
                                            start=j == 0, stop=j == EPC - 1)
                        ins.then_inc(slot_done, 1)
                    if t in (10, 11) and s.runs(3):
                        g, i = s.group(3), t - 10
                        pe.wait_ge(spread_made, g + 1)
                        if i == 1:
                            pe.wait_ge(slot_copied, g + 1)
                        pe.matmul(pD[i][0:LC, 0:SLOTS], img_sel[:, i, :], spread[:, :, :].rearrange("p e k -> p (e k)"),
                                  start=True, stop=True).then_inc(bc_done, 1)
                    if t in (13, 14) and s.runs(3):
                        g, i = s.group(3), t - 13
                        pe.wait_ge(hotG_made, 2 * (G * g + i + 1))
                        for c in range(2):
                            ins = pe.matmul(pD[i][:, 0:SLOTS], xn2[s.parity(3)][:, 2 * i + c, :], hotG[:, 2 * i + c, :],
                                            start=c == 0, stop=c == 1)
                        ins.then_inc(xg_done, 1)
                    if t in (15, 16, 18, 19) and s.runs(3):
                        g, layer, a = s.group(3), int(t > 16), (t - 15) % 3
                        wt, bt, src, done = ((w1s, b1s, XG, m1_done), (w2s, b2s, HID, m2_done))[layer]
                        if layer == 0:
                            pe.wait_ge(xg_copied, G * (g + 1))
                        else:
                            pe.wait_ge(gelu_made, 2 * g + a + 1)
                        pe.matmul(pD[a][:, 0:SLOTS], bt[:, :],
                                  ident[0:NX, NX // 2 * a:NX // 2 * (a + 1)].rearrange("p (e k) -> p e k", k=1)
                                  .broadcast_to([NX, NX // 2, G * CAP]),
                                  start=True, stop=False)
                        for n in range(NX // 2):
                            e = NX // 2 * a + n
                            rhs = src[:, e, :, :].rearrange("p i k -> p (i k)") if layer == 0 else src[:, e, :]
                            ins = pe.matmul(pD[a][:, G * CAP * n:G * CAP * (n + 1)], wt[:, e, :], rhs,
                                            start=False, stop=n == NX // 2 - 1)
                        ins.then_inc(done, 1)
                    if t in (20, 21) and s.runs(3):
                        g, i = s.group(3), t - 20
                        pe.wait_ge(xe_copied, 2 * (g + 1))
                        for c in range(NSC):
                            ins = pe.transpose(pD[i][0:SC, D * c:D * c + D],
                                               XE[:, i, EPC * c:EPC * (c + 1), :].rearrange("p e k -> p (e k)"),
                                               ident[:, :])
                        ins.then_inc(xs_done, 1)
                    if t in (23, 24) and s.runs(3):
                        g, i = s.group(3), t - 23
                        pe.wait_ge(xs_copied, G * g + G)
                        pe.wait_ge(hotS_made, G * NSC * (g + 1))
                        for c in range(2):
                            r = 2 * i + c
                            dst = pD[0][0:LC, r * D:r * D + D]
                            pe.matmul(dst, ident[0:LC, 0:LC], H1[s.parity(3)][:, r, :], start=True, stop=False)
                            for n in range(NSC):
                                ins = pe.matmul(dst, hotS[:, i, n, LC * c:LC * c + LC], XS[:, i, n, :],
                                                start=False, stop=n == NSC - 1)
                        if i == 1:
                            ins.then_inc(y_done, 1)

                    if m.valid:
                        pe.wait_ge(prob_made, m.n + 1)
                        pe.wait_ge(pt_copied, past(m.n - 1))
                        for c in range(2):
                            ins = pe.transpose(pT[m.par][0:LC, 128 * c:128 * c + 128],
                                               prob[:, m.par, LC * c:LC * c + LC], ident[:, :])
                        ins.then_inc(pt_done, 1)

            all_steps(body, pe)


_INS = ['x', 'cls_tok', 'L0_tok_W', 'L0_tok_b', 'L0_tok_token', 'L0_tok_pos', 'L0_attn_Wq', 'L0_attn_bq',
        'L0_attn_Wk', 'L0_attn_bk', 'L0_attn_Wv', 'L0_attn_bv', 'L0_attn_Wo', 'L0_attn_bo',
        'L0_ffn_gate_weight', 'L0_ffn_w1', 'L0_ffn_b1', 'L0_ffn_w2', 'L0_ffn_b2']
_OUT = (64, 198, 128)


def kernel(**inputs):
    import numpy as _np
    import concourse.bacc as _bacc
    from concourse import mybir as _mybir
    from concourse.bass_utils import run_bass_kernel_spmd as _run

    nc = _bacc.Bacc("TRN2", target_bir_lowering=False, num_devices=1)
    arrays, args = {}, []
    for name in _INS:
        a = _np.ascontiguousarray(inputs[name])
        arrays[f"in_{name}_dram"] = a
        args.append(nc.dram_tensor(f"in_{name}_dram", a.shape, _mybir.dt.from_np(a.dtype), kind="ExternalInput").ap())
    out = nc.dram_tensor("out_dram", _OUT, _mybir.dt.float32, kind="ExternalOutput").ap()
    vit_block(nc, *args, out)
    r = _run(nc, [arrays], core_ids=[0])
    return r.results[0]["out_dram"]
```

```python
import concourse.bass as bass
from concourse import mybir
from contextlib import ExitStack



def vit_block(nc, x, cls_tok, tok_W, tok_b, tok_token, tok_pos, Wq, bq, Wk, bk, Wv, bv, Wo, bo,
              gate_weight, w1, b1, w2, b2, out):
    f32 = mybir.dt.float32
    bf16 = mybir.dt.bfloat16
    u32 = mybir.dt.uint32
    ALU = mybir.AluOpType
    ACT = mybir.ActivationFunctionType
    AX = mybir.AxisListType

    B, C, IMG, _ = x.shape
    D = tok_W.shape[0]
    P = 14
    NP = IMG // P
    L = NP * NP + 2
    LC = L // 2
    H = 8
    E = D // H
    NX = gate_weight.shape[1]
    KEEP = 26
    CAP = L // NX * 2
    SLOTS = NX * CAP
    EPC = 4
    NSC = NX // EPC
    SC = EPC * CAP
    G = 2
    NG = B // G
    R = G * 2
    SH = 3
    CP = C * P
    QS = -(-P // SH)
    XPAD = 2 * P
    NEG = -3.4028234663852886e38
    EPS = 1e-5

    TILES = [("tail", 0, 0)]
    for i in range(G):
        TILES += [("full", i, h) for h in range(H)]
        TILES += [("half", i, h) for h in range(0, H, 2)]
    T = len(TILES)
    PAIRS = T // 2 + 1
    NT = T * NG
    TAILR = 64 // H
    NB = 5
    QPARTS = ((0, 128, 0), (H * 128, 64, 128), (H * 192, TAILR, L - TAILR))
    PE_LAG = 6
    HOT_SLOTS = (15, 16, 19, 20, 22, 23)
    EV_LAG = 5
    assert L == 198 and T == 25 and T % NB == 0 and G * H * TAILR == 128

    with ExitStack() as ctx:
        def sb(name, shape, dt=f32):
            return ctx.enter_context(nc.sbuf_tensor(name, shape, dt))

        def ps(name, shape):
            return ctx.enter_context(nc.psum_tensor(name, shape, f32))

        def sem(name):
            return ctx.enter_context(nc.semaphore(name))

        def sb2(name, shape, dt=f32):
            return [sb(f"{name}{p}", shape, dt) for p in range(2)]

        ident = sb("ident", [128, 128])
        ones3 = sb("ones3", [96, LC], bf16)
        tokWT = sb("tokWT", [SH * CP, QS, D])
        posb = sb("posb", [LC, 2, D])
        eye_img = sb("eye_img", [G * NX, G])
        WT = sb("WT", [D, 4, D])
        bcol = sb("bcol", [D, 3])
        bq4 = sb("bq4", [D, 1])
        bias3 = sb("bias3", [96, 3, D], bf16)
        exp_sel = sb("exp_sel", [96, NX], bf16)
        gw = sb("gw", [D, NX])
        w1s = sb("w1s", [D, NX, D])
        w2s = sb("w2s", [D, NX, D])
        img_sel = sb("img_sel", [G * NX, G, LC], bf16)
        own_exp = sb("own_exp", [G * NX, NX])
        slot_sel = sb("slot_sel", [CAP, EPC, SC])
        tok_iota = sb("tok_iota", [SC, L])
        tok_id = sb("tok_id", [LC, 2])
        eps_col = sb("eps_col", [LC, 1])

        X = sb("X", [SH * CP, G, XPAD + NP * IMG])
        Hs = sb("Hs", [LC, R, D])
        xn = sb("xn", [LC, R, D])
        xnT = sb("xnT", [D, G, L])
        QT = sb("QT", [D, G, L])
        QM = sb2("QM", [D, G, H * (128 + 64 + TAILR)])
        KT = sb2("KT", [D, G, L])
        V = sb2("V", [LC, R, D])
        VP = sb("VP", [LC, R, H, 2 * E])
        stats = sb("stats", [LC, R, 6])
        mv = sb("mv", [LC, R, 2])
        rstd = sb("rstd", [LC, 5, R])
        top = sb("top", [128, NB, 7 * 8])
        left = sb("left", [128, NB, L])
        ex = sb("ex", [128, NB, L])
        nmax = sb("nmax", [128, NB])
        extop = sb("extop", [128, KEEP])
        rsum = sb("rsum", [128, NB])
        rinv = sb("rinv", [128, NB])
        prob = sb("prob", [128, NB, L])
        PT = [sb(f"PT{p}", [128, G, 2, H, L]) for p in range(2)]
        setup_room = PT[1][:, 0, :, :, :].rearrange("p c h l -> p (c h l)")
        wload = setup_room[:, 0:C * P * P]
        wraw = setup_room[:, 768:768 + 4 * D].rearrange("p (n d) -> p n d", n=4)
        wsort = setup_room[:, 1792:1792 + C * P * P]
        biasr = setup_room[0:LC, 1536:1536 + 2 * D].rearrange("p (c d) -> p c d", c=2)
        braw = setup_room[0:96, 2560:2560 + 3 * D].rearrange("p (n d) -> p n d", n=3)
        setup_room2 = PT[1][:, 1, :, :, :].rearrange("p c h l -> p (c h l)")
        brest = setup_room2[0:96, 0:3 * D].rearrange("p (n d) -> p n d", n=3)
        bpart = sb("bpart", [96, 3, D], bf16)
        HR = sb2("HR", [LC, R, D])
        OT = sb("OT", [D, G, L])
        H1 = sb2("H1", [LC, R, D])
        xn2 = sb2("xn2", [LC, R, D])
        xn2T = sb("xn2T", [D, G, L])
        stats2 = sb("stats2", [LC, R, 6])
        mv2 = sb("mv2", [LC, R, 2])
        rstd2 = sb("rstd2", [LC, 5, R])
        lmax = sb("lmax", [LC, R])
        lsh = sb("lsh", [LC, R, NX])
        lex = sb("lex", [LC, R, NX])
        lsum = sb("lsum", [LC, R])
        linv = sb("linv", [LC, R])
        aff = sb("aff", [LC, 2, G, NX])
        affT = sb("affT", [G * NX, 3, L])
        route = sb("route", [G * NX, 2, CAP])
        idxu = sb("idxu", [G * NX, CAP], u32)
        routeT = sb("routeT", [CAP, 2, G, NSC, EPC])
        spread = sb("spread", [G * NX, NX, CAP], bf16)
        slotv = sb("slotv", [SC, 2, G, NSC])
        hotG = sb("hotG", [LC, R, SLOTS])
        hotS = sb("hotS", [SC, G, NSC, L])
        XG = sb("XG", [D, NX, G, CAP])
        HID = sb("HID", [D, NX, G * CAP])
        XE = XG[:, :, :, :].rearrange("p e i k -> p (e i k)").rearrange("p (i e k) -> p i e k", i=G, e=NX)
        XS = hotG[0:SC, :, :].rearrange("p r s -> p (r s)")[:, 0:G * NSC * D] \
            .rearrange("p (i c d) -> p i c d", i=G, c=NSC)
        Y = sb("Y", [LC, R, D])

        pS = [ps(f"pS{p}", [128, 512]) for p in range(2)]
        pT = [ps(f"pT{p}", [128, 512]) for p in range(2)]
        pO = ps("pO", [128, 512])
        pA = ps("pA", [128, 512])
        pD = [ps(f"pD{p}", [128, 512]) for p in range(2)]

        w_loaded = sem("w_loaded")
        ident_ready = sem("ident_ready")
        const_step = sem("const_step")
        zero_ready = sem("zero_ready")
        wsorted = sem("wsorted")
        bias_split = sem("bias_split")
        exp_sel_step = sem("exp_sel_step")
        wt_done = sem("wt_done")
        wt_copied = sem("wt_copied")
        posb_ready = sem("posb_ready")
        bq4_ready = sem("bq4_ready")
        x_loaded = sem("x_loaded")
        q_spread = [sem(f"q_spread{p}") for p in range(2)]
        hr_copied = sem("hr_copied")
        vp_made = sem("vp_made")
        stored = sem("stored")
        embedded = sem("embedded")
        h_copied = sem("h_copied")
        stat_step = sem("stat_step")
        var_exp = sem("var_exp")
        newton = sem("newton")
        xn_made = sem("xn_made")
        xnT_done = sem("xnT_done")
        xnT_copied = sem("xnT_copied")
        q_done = sem("q_done")
        q_copied = sem("q_copied")
        k_done = sem("k_done")
        k_copied = sem("k_copied")
        v_done = sem("v_done")
        v_copied = sem("v_copied")
        scored = sem("scored")
        top_found = [sem(f"top_found{r}") for r in range(4)]
        taken = [sem(f"taken{r}") for r in range(4)]
        nmax_made = sem("nmax_made")
        exp_made = sem("exp_made")
        sum_made = sem("sum_made")
        inv_made = sem("inv_made")
        kept_made = sem("kept_made")
        prob_made = sem("prob_made")
        pt_done = sem("pt_done")
        pt_copied = sem("pt_copied")
        pv_done = sem("pv_done")
        o_copied = sem("o_copied")
        proj_done = sem("proj_done")
        h1_copied = sem("h1_copied")
        stat2_step = sem("stat2_step")
        var2_exp = sem("var2_exp")
        newton2 = sem("newton2")
        xn2_made = sem("xn2_made")
        xn2T_done = sem("xn2T_done")
        xn2T_copied = sem("xn2T_copied")
        logit_done = sem("logit_done")
        lmax_made = sem("lmax_made")
        lsh_made = sem("lsh_made")
        lex_made = sem("lex_made")
        lsum_made = sem("lsum_made")
        linv_made = sem("linv_made")
        aff_made = sem("aff_made")
        affT_done = sem("affT_done")
        affT_copied = sem("affT_copied")
        route_step = sem("route_step")
        routed = sem("routed")
        routeT_done = sem("routeT_done")
        routeT_copied = sem("routeT_copied")
        spread_made = sem("spread_made")
        slot_done = sem("slot_done")
        slot_copied = sem("slot_copied")
        bc_done = sem("bc_done")
        hotG_made = sem("hotG_made")
        hotS_made = sem("hotS_made")
        xg_done = sem("xg_done")
        xg_copied = sem("xg_copied")
        m1_done = sem("m1_done")
        gelu_made = sem("gelu_made")
        m2_done = sem("m2_done")
        xe_copied = sem("xe_copied")
        xs_done = sem("xs_done")
        xs_copied = sem("xs_copied")
        y_done = sem("y_done")
        y_copied = sem("y_copied")

        N_W_LOADS = 26

        class Step:

            def __init__(self, half, par):
                self.half, self.par = half, par
                self.k = 2 * half + par

            def known(self):
                return isinstance(self.half, int)

            def runs(self, lag):
                return not self.known() or 0 <= self.k - lag < NG

            def group(self, lag):
                return self.k - lag

            def parity(self, lag):
                return (self.par - lag) % 2

            def rounds(self, lag):
                p = self.parity(lag)
                return self.half + (self.par - lag - p) // 2

            def tile(self, t):
                return Tile(self, t)

        class Tile:
            def __init__(self, step, t):
                back = t < 0
                self.n = (step.k - 1) * T + t
                self.valid = not step.known() or 0 <= self.n < NT
                self.par = ((step.par - 1) * T + t) % 2
                self.buf = t % NB
                self.gpar = step.parity(2 if back else 1)
                self.group = step.k - (2 if back else 1)
                self.t = t % T
                self.kind, self.img, self.head = TILES[self.t]
                pair = (self.t + 1) // 2
                self.pairs = self.group * PAIRS + pair
                self.bank = (self.gpar + pair) % 2
                self.side = (self.t + 1) % 2 if self.t else 0
                self.pair_starts = self.t == 0 or self.t % 2 == 1
                self.pair_ends = self.t % 2 == 0

        def past(count):
            return max(count, 0) if isinstance(count, int) else count

        def settle(eng, *values):
            for v in values:
                if not isinstance(v, int):
                    eng.compute_val(v)
            eng.wait_ge(const_step, 1)

        def all_steps(body, eng):
            for k in range(6):
                body(Step(k // 2, k % 2))
            with eng.Fori(3, NG // 2 - 1) as half:
                body(Step(half, 0))
                body(Step(half, 1))
            for k in range(NG - 2, NG + 4):
                body(Step(k // 2, k % 2))

        block = ctx.enter_context(nc.Block())

        @block.sync
        def _(sp):
            def load_x(s):
                g = s.group(-1)
                sp.wait_ge(embedded, past(g))
                for i in range(G):
                    for sh in range(SH):
                        for c in range(C):
                            src = x[G * g + i, c].rearrange("(n p) w -> p n w", p=P)[:, :, sh:IMG] \
                                if s.known() else \
                                x[bass.ds(G * g + i, 1), c].rearrange("a (n p) w -> (a p) n w", p=P)[:, :, sh:IMG]
                            lo = (sh * C + c) * P
                            dst = X[lo:lo + P, i, XPAD:].rearrange("p (n w) -> p n w", n=NP)
                            sp.dma_start(dst[:, :, 0:IMG - sh], src).then_inc(x_loaded, 16)

            sp.wait_ge(zero_ready, 2)
            load_x(Step(-1, 1))
            sp.dma_start(wload[:, :], tok_W[:, :]).then_inc(w_loaded, 16)
            for n, w in enumerate((Wq, Wk, Wv, Wo)):
                sp.dma_start(wraw[:, n, :], w[:, :]).then_inc(w_loaded, 16)
            for n, v in enumerate((bq, bk, bv)):
                sp.dma_start(bcol[:, n:n + 1], v.rearrange("(p a) -> p a", a=1)).then_inc(w_loaded, 16)
            brow = tok_b.rearrange("(a n) -> a n", a=1)
            sp.dma_start(posb[1:LC, 0, :], tok_pos[0:LC - 1, :]).then_inc(w_loaded, 16)
            sp.dma_start(posb[:, 1, :], tok_pos[LC - 1:L - 1, :]).then_inc(w_loaded, 16)
            sp.dma_start(biasr[0:1, 0, :], cls_tok[0, :, :]).then_inc(w_loaded, 16)
            sp.dma_start(biasr[1:2, 0, :], tok_token[:, :]).then_inc(w_loaded, 16)
            sp.dma_start(biasr[2:LC, 0, :], brow.broadcast_to([LC - 2, D])).then_inc(w_loaded, 16)
            sp.dma_start(biasr[:, 1, :], brow.broadcast_to([LC, D])).then_inc(w_loaded, 16)
            for part in range(3):
                sp.dma_start(braw[32 * part:32 * part + NX, 0, :], b1[:, :]).then_inc(w_loaded, 16)
                sp.dma_start(braw[32 * part:32 * part + NX, 1, :], b2[:, :]).then_inc(w_loaded, 16)
                sp.dma_start(braw[32 * part:32 * part + 1, 2, :], bo.rearrange("(a n) -> a n", a=1)).then_inc(w_loaded, 16)
            sp.dma_start(gw[:, :], gate_weight[:, :]).then_inc(w_loaded, 16)
            sp.dma_start(w1s[:, :, :], w1.rearrange("e d f -> d e f")).then_inc(w_loaded, 16)
            sp.dma_start(w2s[:, :, :], w2.rearrange("e f d -> f e d")).then_inc(w_loaded, 16)

            def body(s):
                if s.runs(1):
                    p = s.parity(1)
                    settle(sp, s.group(1) + 1, s.group(1) - 1)
                    sp.wait_ge(h_copied, s.group(1) + 1)
                    sp.wait_ge(proj_done, past(s.group(1) - 1))
                    sp.dma_start(HR[p][:, :, :], Hs[:, :, :]).then_inc(hr_copied, 16)
                if s.runs(-1):
                    load_x(s)
                if s.runs(0):
                    p = s.parity(0)
                    settle(sp, s.group(0) + 1, (s.group(0) - 1) * T)
                    sp.wait_ge(q_copied, s.group(0) + 1)
                    sp.wait_ge(scored, past((s.group(0) - 1) * T))
                    for h in range(H):
                        rows = slice(h * E, h * E + E)
                        for base, n, lo in QPARTS:
                            sp.dma_start(QM[p][rows, :, base + n * h:base + n * (h + 1)], QT[rows, :, lo:lo + n]) \
                              .then_inc(q_spread[p], 16)
                if s.runs(4):
                    g = s.group(4)
                    sp.wait_ge(y_copied, g + 1)
                    dst = out[G * g:G * g + G] if s.known() else out[bass.ds(G * g, G)]
                    sp.dma_start(dst.rearrange("b (c p) d -> p b c d", p=LC),
                                 Y[:, :, :].rearrange("p (b c) d -> p b c d", b=G)) \
                      .then_inc(stored, 16)

            all_steps(body, sp)
            sp.wait_ge(stored, 16 * NG)

        @block.gpsimd
        def _(pool):
            pool.memset(X[:, :, 0:XPAD], 0.0)
            pool.memset(ident[:, :], 0.0).then_inc(const_step, 1)
            pool.memset(braw[:, :, :], 0.0)
            pool.memset(posb[:, :, :], 0.0).then_inc(zero_ready, 2)
            pool.wait_ge(const_step, 1)
            pool.affine_select(out=ident[:, :], in_=ident[:, :], compare_op=ALU.not_equal, fill=1.0,
                               base=0, pattern=[[-1, 128]], channel_multiplier=1).then_inc(ident_ready, 1)
            pool.memset(VP[:, :, :, :], 0.0)
            for p in range(2):
                pool.memset(QM[p][:, :, :], 0.0).then_inc(zero_ready, 1)
            pool.memset(ones3[:, :], 1.0)
            pool.memset(exp_sel[:, :], 0.0)
            pool.memset(eps_col[:, :], EPS)
            pool.memset(img_sel[:, :, :], 1.0)
            pool.memset(own_exp[:, :], 0.0)
            pool.memset(slot_sel[:, :, :], 0.0)
            pool.memset(top[:, :, :], NEG)
            pool.iota(tok_iota[:, :], pattern=[[1, L]], base=0, channel_multiplier=0,
                      allow_small_or_imprecise_dtypes=True)
            pool.iota(tok_id[:, :], pattern=[[LC, 2]], base=0, channel_multiplier=1,
                      allow_small_or_imprecise_dtypes=True).then_inc(const_step, 1)
            pool.wait_ge(const_step, 2)
            for i in range(G):
                pool.affine_select(out=own_exp[:, :], in_=own_exp[:, :], compare_op=ALU.not_equal, fill=1.0,
                                   base=-NX * i, pattern=[[-1, NX]], channel_multiplier=1) \
                    .then_inc(const_step, 1)
                pool.wait_ge(const_step, 3 + i)
            for part in range(3):
                pool.affine_select(out=exp_sel[:, :], in_=exp_sel[:, :], compare_op=ALU.not_equal, fill=1.0,
                                   base=-32 * part, pattern=[[-1, NX]], channel_multiplier=1) \
                    .then_inc(exp_sel_step, 1)
                pool.wait_ge(exp_sel_step, part + 1)
            pool.affine_select(out=slot_sel[:, :, :], in_=slot_sel[:, :, :], compare_op=ALU.not_equal, fill=1.0,
                               base=0, pattern=[[CAP, EPC], [-1, SC]], channel_multiplier=1)
            pool.affine_select(out=img_sel[:, :, :], in_=img_sel[:, :, :], compare_op=ALU.is_ge, fill=0.0,
                               base=0, pattern=[[-NX, G], [0, LC]], channel_multiplier=1) \
                .then_inc(const_step, 1)
            pool.wait_ge(const_step, 3 + G)
            pool.affine_select(out=img_sel[:, :, :], in_=img_sel[:, :, :], compare_op=ALU.is_ge, fill=0.0,
                               base=NX - 1, pattern=[[NX, G], [0, LC]], channel_multiplier=-1) \
                .then_inc(const_step, 1)

            def refine(mvt, r, exped, done, n):
                var = mvt[:, :, 1]
                settle(pool, 2 * n + 2)
                pool.wait_ge(exped, 2 * n + 2)
                pool.tensor_tensor(r[:, 4, :], r[:, 1, :], r[:, 1, :], ALU.mult).then_inc(done, 1)
                pool.tensor_scalar(r[:, 0, :], var, EPS, -0.5, ALU.add, ALU.mult).then_inc(done, 1)
                pool.wait_ge(done, 7 * n + 2)
                pool.tensor_tensor(r[:, 4, :], r[:, 4, :], r[:, 0, :], ALU.mult).then_inc(done, 1)
                settle(pool, 7 * n + 3)
                pool.wait_ge(done, 7 * n + 3)
                pool.tensor_scalar(r[:, 4, :], r[:, 4, :], 1.5, None, ALU.add).then_inc(done, 1)
                pool.wait_ge(done, 7 * n + 4)
                pool.tensor_tensor(r[:, 2, :], r[:, 4, :], r[:, 1, :], ALU.mult).then_inc(done, 1)
                pool.wait_ge(done, 7 * n + 5)
                pool.tensor_tensor(r[:, 3, :], mvt[:, :, 0], r[:, 2, :], ALU.mult).then_inc(done, 1)
                settle(pool, 7 * n + 6)
                pool.wait_ge(done, 7 * n + 6)
                pool.tensor_scalar(r[:, 3, :], r[:, 3, :], -1.0, None, ALU.mult).then_inc(done, 1)

            def body(s):
                for t in range(T):
                    if t == 10 and s.runs(0):
                        refine(mv, rstd, var_exp, newton, s.group(0))
                    if t == 17 and s.runs(2):
                        refine(mv2, rstd2, var2_exp, newton2, s.group(2))
                    if t == 4 and s.runs(2):
                        g = s.group(2)
                        settle(pool, g + 1, g)
                        pool.wait_ge(v_copied, g + 1)
                        pool.wait_ge(pv_done, past(g))
                        for b in range(2):
                            dst = VP[:, :, :, b * E:b * E + E].rearrange("p r (j b) e -> p r j b e", b=2)[:, :, :, b, :]
                            src = V[s.parity(2)][:, :, :].rearrange("p r (j b e) -> p r j b e", b=2, e=E)[:, :, :, b, :]
                            pool.tensor_copy(dst, src).then_inc(vp_made, 1)
                    if t == 3 and s.runs(3):
                        g = s.group(3)
                        pool.wait_ge(linv_made, g + 1)
                        pool.wait_ge(affT_done, past(g))
                        pool.tensor_tensor(aff[:, :, :, :].rearrange("p c i e -> p i c e"),
                                           lex[:, :, :].rearrange("p (i c) e -> p i c e", i=G),
                                           linv[:, :].rearrange("p (i c a) -> p i c a", i=G, a=1)
                                           .broadcast_to([LC, G, 2, NX]), ALU.mult).then_inc(aff_made, 1)
                    if t == 10 and s.runs(3):
                        g = s.group(3)
                        pool.wait_ge(routed, g + 1)
                        pool.wait_ge(bc_done, past(G * g))
                        pool.tensor_tensor(spread[:, :, :],
                                           route[:, 0:1, :].broadcast_to([G * NX, NX, CAP]),
                                           own_exp[:, :].rearrange("p (e a) -> p e a", a=1)
                                           .broadcast_to([G * NX, NX, CAP]), ALU.mult).then_inc(spread_made, 1)
                    late = t in (0, 2)
                    if (late and s.runs(4)) or (t in HOT_SLOTS and s.runs(3)):
                        g, n = s.group(4 if late else 3), 6 + t // 2 if late else HOT_SLOTS.index(t)
                        i, c = divmod(n, NSC)
                        settle(pool, g + 1, g)
                        pool.wait_ge(slot_copied, g + 1)
                        pool.wait_ge(y_done, past(g))
                        pool.tensor_scalar(hotS[:, i, c, :], tok_iota[:, :], slotv[:, 0, i, c:c + 1],
                                           slotv[:, 1, i, c:c + 1], ALU.is_equal, ALU.mult).then_inc(hotS_made, 1)
                    q = s.tile(t - 2)
                    if q.valid:
                        settle(pool, q.n + 1, q.n - NB + 1)
                        pool.wait_ge(inv_made, q.n + 1)
                        pool.wait_ge(taken[3], q.n + 1)
                        pool.tensor_scalar(left[:, q.buf, :], left[:, q.buf, :], NEG, rinv[:, q.buf:q.buf + 1],
                                           ALU.is_equal, ALU.mult).then_inc(kept_made, 1)
                        pool.wait_ge(kept_made, q.n + 1)
                        pool.wait_ge(exp_made, q.n + 1)
                        pool.wait_ge(pt_done, past(q.n - NB + 1))
                        pool.tensor_tensor(prob[:, q.buf, :], left[:, q.buf, :], ex[:, q.buf, :], ALU.mult) \
                            .then_inc(prob_made, 1)

            all_steps(body, pool)

        @block.vector
        def _(dve):
            dve.wait_ge(w_loaded, 16 * N_W_LOADS)
            dve.wait_ge(zero_ready, 2)
            dve.tensor_tensor(posb[:, :, :], posb[:, :, :], biasr[:, :, :], ALU.add).then_inc(posb_ready, 1)
            dve.tensor_copy(bpart[:, :, :], braw[:, :, :]).then_inc(bias_split, 1)
            dve.wait_ge(bias_split, 1)
            dve.tensor_copy(bias3[0:32, :, :], bpart[0:32, :, :]).then_inc(bias_split, 1)
            dve.tensor_tensor(brest[:, :, :], braw[:, :, :], bpart[:, :, :], ALU.subtract).then_inc(bias_split, 1)
            dve.wait_ge(bias_split, 3)
            dve.tensor_copy(bpart[:, :, :], brest[:, :, :]).then_inc(bias_split, 1)
            dve.wait_ge(bias_split, 4)
            dve.tensor_copy(bias3[32:64, :, :], bpart[32:64, :, :]).then_inc(bias_split, 1)
            dve.tensor_tensor(brest[:, :, :], brest[:, :, :], bpart[:, :, :], ALU.subtract).then_inc(bias_split, 1)
            dve.wait_ge(bias_split, 6)
            dve.tensor_copy(bias3[64:96, :, :], brest[64:96, :, :]).then_inc(bias_split, 1)
            dve.wait_ge(const_step, 4 + G)

            def found(q, r):
                settle(dve, q.n + 1, q.n - NB + 1)
                if r == 0:
                    dve.wait_ge(scored, q.n + 1)
                    dve.wait_ge(inv_made, past(q.n - NB + 1))
                else:
                    dve.wait_ge(taken[r - 1], q.n + 1)
                src = pS[q.par][:, 0:L] if r == 0 else left[:, q.buf, :]
                dve.max(top[:, q.buf, 8 * r:8 * r + 8], src).then_inc(top_found[r], 1)

            def take(q, r):
                settle(dve, q.n + 1, q.n - NB + 1)
                dve.wait_ge(top_found[r], q.n + 1)
                if r == 0:
                    dve.wait_ge(prob_made, past(q.n - NB + 1))
                src = pS[q.par][:, 0:L] if r == 0 else left[:, q.buf, :]
                what = top[:, q.buf, 8 * r:8 * r + 8]
                if r == 3:
                    what = top[:, q.buf, 24:56].rearrange("p (a b) -> p a b", b=8)[:, :, 0:2]
                dve.match_replace(left[:, q.buf, :], what, src, NEG).then_inc(taken[r], 1)

            def layer_stats(src, ready, st, mvt, step, refined, n):
                dve.wait_ge(ready, n + 1)
                dve.wait_ge(refined, past(7 * n))
                for r in range(R):
                    dve.bn_stats(st[:, r, :], src[:, r, :]).then_inc(step, 1)

            def layer_moments(st, mvt, step, n):
                settle(dve, 2 * R * n + R)
                dve.wait_ge(step, 2 * R * n + R)
                for r in range(R):
                    dve.bn_aggr(mvt[:, r, :], st[:, r, :]).then_inc(step, 1)

            def between(s, t):
                if t == 9 and s.runs(0):
                    layer_moments(stats, mv, stat_step, s.group(0))
                if t == 15 and s.runs(2):
                    layer_moments(stats2, mv2, stat2_step, s.group(2))
                if t == 1 and s.runs(3):
                    g = s.group(3)
                    dve.wait_ge(lmax_made, g + 1)
                    dve.wait_ge(lex_made, past(g))
                    dve.tensor_tensor(lsh[:, :, :], pO[0:LC, 0:R * NX].rearrange("p (r e) -> p r e", r=R),
                                      lmax[:, :].rearrange("p (r a) -> p r a", a=1).broadcast_to([LC, R, NX]),
                                      ALU.subtract).then_inc(lsh_made, 1)
                if t == 3 and s.runs(3):
                    g = s.group(3)
                    dve.wait_ge(lsum_made, g + 1)
                    dve.wait_ge(aff_made, past(g))
                    dve.reciprocal(linv[:, :], lsum[:, :]).then_inc(linv_made, 1)
                if t in (7, 8, 9) and s.runs(3):
                    g, r = s.group(3), t - 7
                    n = 8 * g + 3 * r
                    m = route[:, 1, 8 * r:8 * r + 8]
                    settle(dve, n + 1)
                    dve.wait_ge(route_step, n + 1)
                    dve.max_index(idxu[:, 8 * r:8 * r + 8], m, affT[:, r, :]).then_inc(route_step, 1)
                    if r < 2:
                        dve.match_replace(affT[:, r + 1, :], m, affT[:, r, :], NEG).then_inc(route_step, 1)

            def body(s):
                for t in range(T):
                    q, o, f = s.tile(t), s.tile(t - 1), s.tile(t - 2)
                    if q.valid:
                        found(q, 0)
                    if o.valid:
                        found(o, 2)
                    between(s, t)
                    if q.valid:
                        take(q, 0)
                    if o.valid:
                        take(o, 2)
                    if f.valid:
                        dve.wait_ge(sum_made, f.n + 1)
                        dve.wait_ge(kept_made, past(f.n - NB + 1))
                        dve.reciprocal(rinv[:, f.buf:f.buf + 1], rsum[:, f.buf:f.buf + 1]).then_inc(inv_made, 1)
                    if q.valid:
                        dve.wait_ge(exp_made, past(q.n - NB + 1))
                        dve.tensor_scalar(nmax[:, q.buf:q.buf + 1], top[:, q.buf, 0:1], -1.0, None, ALU.mult) \
                           .then_inc(nmax_made, 1)
                        found(q, 1)
                    if o.valid:
                        found(o, 3)
                    if q.valid:
                        take(q, 1)
                    if o.valid:
                        take(o, 3)

                    if t == 8 and s.runs(0):
                        layer_stats(Hs, h_copied, stats, mv, stat_step, newton, s.group(0))
                    if t == 14 and s.runs(2):
                        layer_stats(H1[s.parity(2)], h1_copied, stats2, mv2, stat2_step, newton2, s.group(2))
                    if t == 0 and s.runs(3):
                        g = s.group(3)
                        lg = pO[0:LC, 0:R * NX].rearrange("p (r e) -> p r e", r=R)
                        dve.wait_ge(logit_done, g + 1)
                        dve.tensor_reduce(lmax[:, :], lg, axis=AX.X, op=ALU.max).then_inc(lmax_made, 1)
                    if t == 2 and s.runs(3):
                        g = s.group(3)
                        dve.wait_ge(lex_made, g + 1)
                        dve.tensor_reduce(lsum[:, :], lex[:, :, :], axis=AX.X, op=ALU.add).then_inc(lsum_made, 1)
                    if t in (6, 7, 8) and s.runs(3):
                        g, r = s.group(3), t - 6
                        n = 8 * g + 3 * r
                        settle(dve, g + 1, g, n)
                        if r == 0:
                            dve.wait_ge(affT_copied, g + 1)
                            dve.wait_ge(spread_made, past(g))
                            dve.wait_ge(routeT_done, past(g))
                        else:
                            dve.wait_ge(route_step, past(n))
                        dve.max(route[:, 1, 8 * r:8 * r + 8], affT[:, r, :]).then_inc(route_step, 1)
                    if t == 9 and s.runs(3):
                        g = s.group(3)
                        dve.wait_ge(route_step, 8 * g + 8)
                        dve.tensor_copy(route[:, 0, :], idxu[:, :]).then_inc(routed, 1)
                    if t in (14, 16) and s.runs(3):
                        i, g = t // 2 - 7, s.group(3)
                        dve.wait_ge(bc_done, G * g + i + 1)
                        dve.wait_ge(y_done, past(g))
                        for c in range(2):
                            dve.tensor_scalar(hotG[:, 2 * i + c, :], pD[1 - i][0:LC, 0:SLOTS], tok_id[:, c:c + 1], None,
                                              ALU.is_equal).then_inc(hotG_made, 1)

            all_steps(body, dve)

        @block.scalar
        def _(act):
            act.wait_ge(w_loaded, 16 * N_W_LOADS)
            act.activation(wsort.rearrange("d (q c) -> d q c", q=P), wload.rearrange("d (c q) -> d q c", q=P),
                           ACT.Copy).then_inc(wsorted, 1)
            for n in range(QS + 4):
                act.wait_ge(wt_done, n + 1)
                if n < QS:
                    rows = min(SH, P - SH * n) * CP
                    act.activation(tokWT[0:rows, n, :], pT[n % 2][0:rows, 0:D], ACT.Copy).then_inc(wt_copied, 1)
                else:
                    act.activation(WT[:, n - QS, :], pT[n % 2][:, 0:D], ACT.Copy).then_inc(wt_copied, 1)
            act.activation(bq4[:, :], bcol[:, 0:1], ACT.Copy, scale=0.25).then_inc(bq4_ready, 1)
            act.wait_ge(bq4_ready, 1)

            def inv_std(mvt, r, step, exped, refined, n):
                act.wait_ge(step, past(2 * R * n + 2 * R))
                act.wait_ge(refined, past(7 * n))
                act.activation(r[:, 0, :], mvt[:, :, 1], ACT.Ln, bias=eps_col[:, 0:1]).then_inc(exped, 1)
                act.wait_ge(exped, 2 * n + 1)
                act.activation(r[:, 1, :], r[:, 0, :], ACT.Exp, scale=-0.5).then_inc(exped, 1)

            def body(s):
                for t in range(T):
                    q, o, m = s.tile(t), s.tile(t - 1), s.tile(t - EV_LAG)
                    if q.valid:
                        act.wait_ge(nmax_made, q.n + 1)
                        act.wait_ge(taken[0], q.n + 1)
                        act.wait_ge(prob_made, past(q.n - NB + 1))
                        act.activation(ex[:, q.buf, :], pS[q.par][:, 0:L], ACT.Exp, bias=nmax[:, q.buf:q.buf + 1]) \
                           .then_inc(exp_made, 1)
                    if o.valid:
                        act.wait_ge(top_found[3], o.n + 1)
                        act.wait_ge(inv_made, past(o.n - NB + 1))
                        act.wait_ge(sum_made, past(o.n))
                        act.activation(extop[:, :], top[:, o.buf, 0:KEEP], ACT.Exp, bias=nmax[:, o.buf:o.buf + 1],
                                       accum_out=rsum[:, o.buf:o.buf + 1]).then_inc(sum_made, 1)
                    if m.valid and m.pair_ends:
                        act.wait_ge(pt_done, m.n + 1)
                        if m.t == 0:
                            act.wait_ge(pv_done, past(m.group - 1))
                        dst, src = PT[m.gpar][0:LC], pT[m.bank][0:LC, :].rearrange("p (t c r) -> p t c r", t=2, c=2)
                        if m.kind == "full":
                            for c in range(2):
                                ins = act.activation(dst[:, m.img, c, m.head - 1:m.head + 1, 0:128], src[:, :, c, :],
                                                     ACT.Copy)
                        elif m.kind == "half":
                            for c in range(2):
                                ins = act.activation(dst[:, m.img, c, m.head - 2:m.head + 2, 128:192],
                                                     src[:, :, c, :].rearrange("p t (h r) -> p t h r", h=2),
                                                     ACT.Copy)
                        else:
                            for i in range(G):
                                v = src[:, 0, :, 64 * i:64 * i + 64].rearrange("p c (h r) -> p c h r", h=H)
                                ins = act.activation(dst[:, i, :, :, 192:L], v[:, :, :, TAILR - (L - 192):TAILR],
                                                     ACT.Copy)
                        ins.then_inc(pt_copied, 1)

                    if t == 5 and s.runs(3):
                        g = s.group(3)
                        act.wait_ge(affT_done, g + 1)
                        act.wait_ge(route_step, past(8 * g))
                        act.activation(affT[:, 0, :], pO[0:G * NX, 0:L], ACT.Copy).then_inc(affT_copied, 1)
                    if t == 7 and s.runs(0):
                        g = s.group(0)
                        act.wait_ge(embedded, g + 1)
                        act.wait_ge(hr_copied, past(16 * g))
                        act.activation(Hs[:, :, :], pA[0:LC, 0:R * D].rearrange("p (r d) -> p r d", r=R), ACT.Copy) \
                           .then_inc(h_copied, 1)
                    if t == 9 and s.runs(0):
                        inv_std(mv, rstd, stat_step, var_exp, newton, s.group(0))
                    if t == 11 and s.runs(0):
                        g = s.group(0)
                        act.wait_ge(newton, 7 * g + 7)
                        act.wait_ge(xnT_done, past(g))
                        for r in range(R):
                            act.activation(xn[:, r, :], Hs[:, r, :], ACT.Identity,
                                           bias=rstd[:, 3, r:r + 1], scale=rstd[:, 2, r:r + 1]).then_inc(xn_made, 1)
                    if t == 11 and s.runs(3):
                        g = s.group(3)
                        act.wait_ge(routeT_done, g + 1)
                        act.wait_ge(slot_done, past(g))
                        act.activation(routeT[:, :, :, :, :],
                                       pD[1][0:CAP, 0:2 * G * NX].rearrange("p (v i c j) -> p v i c j", v=2, i=G, c=NSC),
                                       ACT.Copy).then_inc(routeT_copied, 1)
                    if t == 13 and s.runs(3):
                        g = s.group(3)
                        act.wait_ge(slot_done, g + 1)
                        act.wait_ge(hotS_made, past(G * NSC * g))
                        act.activation(slotv[:, :, :, :],
                                       pD[0][0:SC, 0:2 * G * NSC].rearrange("p (v i c) -> p v i c", v=2, i=G),
                                       ACT.Copy).then_inc(slot_copied, 1)
                    if t == 13 and s.runs(0):
                        g = s.group(0)
                        act.wait_ge(xnT_done, g + 1)
                        act.wait_ge(v_done, past(g))
                        act.activation(xnT[:, :, :], pA[:, 0:G * L].rearrange("p (i l) -> p i l", i=G), ACT.Copy) \
                           .then_inc(xnT_copied, 1)
                    if t == 15 and s.runs(0):
                        p, g = s.parity(-1), s.group(0)
                        act.wait_ge(q_done, g + 1)
                        act.wait_ge(q_spread[p], past(16 * 3 * H * s.rounds(-1)))
                        act.activation(QT[:, :, :], pA[:, 0:G * L].rearrange("p (i l) -> p i l", i=G), ACT.Identity,
                                       bias=bq4[:, 0:1], scale=0.25).then_inc(q_copied, 1)
                    if t == 17 and s.runs(0):
                        p, g = s.parity(0), s.group(0)
                        act.wait_ge(k_done, g + 1)
                        act.activation(KT[p][:, :, :], pA[:, 0:G * L].rearrange("p (i l) -> p i l", i=G), ACT.Identity,
                                       bias=bcol[:, 1:2]).then_inc(k_copied, 1)
                    if t == 19 and s.runs(0):
                        p, g = s.parity(0), s.group(0)
                        act.wait_ge(v_done, g + 1)
                        act.wait_ge(vp_made, past(2 * (g - 1)))
                        act.activation(V[p][:, :, :], pA[0:LC, 0:R * D].rearrange("p (r d) -> p r d", r=R), ACT.Copy) \
                           .then_inc(v_copied, 1)
                    if t in (16, 18) and s.runs(3):
                        g, i = s.group(3), t // 2 - 8
                        act.wait_ge(xg_done, G * g + i + 1)
                        act.wait_ge(xs_done, past(G * g))
                        act.activation(XG[:, :, i, :], pD[1 - i][:, 0:SLOTS].rearrange("p (e k) -> p e k", e=NX), ACT.Copy) \
                           .then_inc(xg_copied, 1)
                    if t == 10 and s.runs(2):
                        g = s.group(2)
                        act.wait_ge(pv_done, g + 1)
                        act.wait_ge(proj_done, past(g))
                        act.activation(OT[:, :, :], pO[:, 0:G * L].rearrange("p (i l) -> p i l", i=G), ACT.Identity,
                                       bias=bcol[:, 2:3]).then_inc(o_copied, 1)
                    if t == 13 and s.runs(2):
                        p, g = s.parity(2), s.group(2)
                        act.wait_ge(proj_done, g + 1)
                        act.wait_ge(y_done, past(g - 1))
                        act.activation(H1[p][:, :, :], pO[0:LC, 0:R * D].rearrange("p (r d) -> p r d", r=R), ACT.Copy) \
                           .then_inc(h1_copied, 1)
                    if t in (22, 24) and s.runs(3):
                        g, a = s.group(3), t // 2 - 11
                        act.wait_ge(m1_done, 2 * g + a + 1)
                        act.wait_ge(m2_done, past(2 * g))
                        act.activation(HID[:, NX // 2 * a:NX // 2 * (a + 1), :],
                                       pD[a][:, 0:SLOTS].rearrange("p (e k) -> p e k", e=NX // 2),
                                       ACT.Gelu_apprx_tanh).then_inc(gelu_made, 1)
                    if t == 16 and s.runs(2):
                        inv_std(mv2, rstd2, stat2_step, var2_exp, newton2, s.group(2))
                    if t in (1, 3) and s.runs(4):
                        g, a = s.group(4), t // 2
                        act.wait_ge(m2_done, 2 * g + a + 1)
                        act.wait_ge(xs_done, past(G * g))
                        act.activation(XE[:, :, NX // 2 * a:NX // 2 * (a + 1), :].rearrange("p i e k -> p e i k"),
                                       pD[a][:, 0:SLOTS].rearrange("p (e i k) -> p e i k", e=NX // 2, i=G),
                                       ACT.Copy).then_inc(xe_copied, 1)
                    if t == 19 and s.runs(2):
                        p, g = s.parity(2), s.group(2)
                        act.wait_ge(newton2, 7 * g + 7)
                        act.wait_ge(xg_done, past(G * (g - 1)))
                        for r in range(R):
                            act.activation(xn2[p][:, r, :], H1[p][:, r, :], ACT.Identity,
                                           bias=rstd2[:, 3, r:r + 1], scale=rstd2[:, 2, r:r + 1]).then_inc(xn2_made, 1)
                    if t == 5 and s.runs(4):
                        g = s.group(4)
                        for i in range(G):
                            act.wait_ge(xs_done, G * g + i + 1)
                            act.wait_ge(y_done, past(g))
                            act.activation(XS[:, i, :, :], pD[i][0:SC, 0:NSC * D].rearrange("p (c d) -> p c d", c=NSC),
                                           ACT.Copy).then_inc(xs_copied, 1)
                    if t == 22 and s.runs(2):
                        g = s.group(2)
                        act.wait_ge(xn2T_done, g + 1)
                        act.wait_ge(logit_done, past(g))
                        act.activation(xn2T[:, :, :], pA[:, 0:G * L].rearrange("p (i l) -> p i l", i=G), ACT.Copy) \
                           .then_inc(xn2T_copied, 1)
                    if t == 2 and s.runs(3):
                        g = s.group(3)
                        act.wait_ge(lsh_made, g + 1)
                        act.wait_ge(aff_made, past(g))
                        act.activation(lex[:, :, :], lsh[:, :, :], ACT.Exp).then_inc(lex_made, 1)
                    if t == 11 and s.runs(4):
                        g = s.group(4)
                        act.wait_ge(y_done, g + 1)
                        act.wait_ge(stored, past(16 * g))
                        act.activation(Y[:, :, :], pD[0][0:LC, 0:R * D].rearrange("p (r d) -> p r d", r=R), ACT.Copy) \
                           .then_inc(y_copied, 1)

            all_steps(body, act)

        @block.tensor
        def _(pe):
            pe.wait_ge(w_loaded, 16 * N_W_LOADS)
            pe.wait_ge(ident_ready, 1)
            pe.wait_ge(wsorted, 1)
            for n in range(QS + 4):
                pe.wait_ge(wt_copied, past(n - 1))
                if n < QS:
                    cols = min(SH, P - SH * n)
                    src = wsort[:, SH * n * CP:(SH * n + cols) * CP]
                    pe.transpose(pT[n % 2][0:cols * CP, 0:D], src, ident[:, :]).then_inc(wt_done, 1)
                else:
                    pe.transpose(pT[n % 2][:, 0:D], wraw[:, n - QS, :], ident[:, :]).then_inc(wt_done, 1)
            pe.wait_ge(wt_copied, QS + 4)
            pe.wait_ge(posb_ready, 1)
            pe.wait_ge(bias_split, 7)
            pe.wait_ge(exp_sel_step, 3)
            pe.wait_ge(const_step, 4 + G)
            pe.wait_ge(zero_ready, 4)

            def chunk(i, c):
                return slice(i * L + c * LC, i * L + (c + 1) * LC)

            def score(q, par):
                pe.wait_ge(exp_made, past(q.n - 1))
                if q.t == 0:
                    pe.wait_ge(k_copied, q.group + 1)
                qm, k = QM[q.gpar], KT[q.gpar]
                dst = pS[q.par]
                if q.kind == "full":
                    pe.matmul(dst[:, 0:L], qm[:, q.img, 128 * q.head:128 * q.head + 128], k[:, q.img, :], start=True, stop=True) \
                      .then_inc(scored, 1)
                elif q.kind == "half":
                    lo = QPARTS[1][0] + 64 * q.head
                    pe.matmul(dst[:, 0:L], qm[:, q.img, lo:lo + 128], k[:, q.img, :],
                              start=True, stop=True).then_inc(scored, 1)
                else:
                    for i in range(G):
                        ins = pe.matmul(dst[64 * i:64 * i + 64, 0:L], qm[:, i, QPARTS[2][0]:], k[:, i, :],
                                        start=True, stop=True)
                    ins.then_inc(scored, 1)

            def experts(layer, a, part, src, done):
                w = (w1s, w2s)[layer]
                if part == 0:
                    pe.matmul(pD[a][:, 0:SLOTS], bias3[:, layer, :],
                              exp_sel[:, NX // 2 * a:NX // 2 * (a + 1)].rearrange("p (e k) -> p e k", k=1)
                              .broadcast_to([96, NX // 2, G * CAP]),
                              start=True, stop=False)
                for n in range(NX // 4 * part, NX // 4 * (part + 1)):
                    e = NX // 2 * a + n
                    rhs = src[:, e, :, :].rearrange("p i k -> p (i k)") if layer == 0 else src[:, e, :]
                    ins = pe.matmul(pD[a][:, G * CAP * n:G * CAP * (n + 1)], w[:, e, :], rhs,
                                    start=False, stop=n == NX // 2 - 1)
                if part == 1:
                    ins.then_inc(done, 1)

            def body(s):
                for t in range(T):
                    q, m = s.tile(t), s.tile(t - PE_LAG)
                    if q.valid:
                        if t == 0:
                            pe.wait_ge(q_spread[q.gpar], 16 * 3 * H * (s.rounds(1) + 1))
                        score(q, s.par)

                    if 2 <= t < 8 and s.runs(0):
                        g = s.group(0)
                        if t == 2:
                            pe.wait_ge(x_loaded, 16 * G * SH * C * (g + 1))
                            pe.wait_ge(v_copied, past(g))
                            pe.wait_ge(xn2T_copied, past(g - 2))
                        for n in range(4 * t - 8, 4 * t - 4):
                            r, part = divmod(n, QS + 1)
                            i, c = divmod(r, 2)
                            dst = pA[0:LC, r * D:r * D + D]
                            if part < QS:
                                kp = min(SH, P - SH * part) * CP
                                lo = XPAD + P * (LC * c - 2) + SH * part
                                src = X[0:kp, i, lo:lo + P * (LC - 1) + 1:P]
                                ins = pe.matmul(dst, src, tokWT[0:kp, part, :], start=part == 0, stop=False)
                            else:
                                ins = pe.matmul(dst, ident[0:LC, 0:LC], posb[:, c, :], start=False, stop=True)
                        if t == 7:
                            ins.then_inc(embedded, 1)
                    if t == 14 and s.runs(0):
                        g = s.group(0)
                        pe.wait_ge(xn_made, R * g + R)
                        for r in range(R):
                            ins = pe.transpose(pA[:, chunk(r // 2, r % 2)], xn[:, r, :], ident[0:LC, 0:LC])
                        ins.then_inc(xnT_done, 1)
                    if t == 16 and s.runs(0):
                        pe.wait_ge(xnT_copied, s.group(0) + 1)
                        pe.matmul(pA[:, 0:G * L], WT[:, 0, :], xnT[:, :, :], start=True, stop=True).then_inc(q_done, 1)
                    if t == 18 and s.runs(0):
                        pe.wait_ge(q_copied, s.group(0) + 1)
                        pe.matmul(pA[:, 0:G * L], WT[:, 1, :], xnT[:, :, :], start=True, stop=True).then_inc(k_done, 1)
                    if t == 20 and s.runs(0):
                        pe.wait_ge(k_copied, s.group(0) + 1)
                        for r in range(R):
                            ins = pe.matmul(pA[0:LC, r * D:r * D + D], xnT[:, r // 2, LC * (r % 2):LC * (r % 2 + 1)],
                                            WT[:, 2, :], start=True, stop=True)
                        ins.then_inc(v_done, 1)

                    if 7 <= t < 11 and s.runs(2):
                        p, g = s.parity(2), s.group(2)
                        if t == 7:
                            pe.wait_ge(affT_copied, past(g))
                            pe.wait_ge(pt_copied, (g + 1) * PAIRS)
                            pe.wait_ge(vp_made, 2 * (g + 1))
                        i, b = divmod(t - 7, 2)
                        for c, j in ((c, j) for c in range(2) for j in range(4)):
                            h = 2 * j + b
                            ins = pe.matmul(pO[32 * j:32 * j + 32, i * L:i * L + L], VP[:, 2 * i + c, h, :],
                                            PT[p][0:LC, i, c, h, :], start=b + c == 0, stop=b + c == 2)
                        if t == 10:
                            ins.then_inc(pv_done, 1)
                    if t == 13 and s.runs(2):
                        p, g = s.parity(2), s.group(2)
                        pe.wait_ge(o_copied, g + 1)
                        pe.wait_ge(hr_copied, 16 * (g + 1))
                        pe.matmul(pO[0:LC, 0:R * D], ones3[:, :], bias3[:, 2:3, :].broadcast_to([96, R, D]),
                                  start=True, stop=False)
                        for r in range(R):
                            dst = pO[0:LC, r * D:r * D + D]
                            pe.matmul(dst, OT[:, r // 2, LC * (r % 2):LC * (r % 2 + 1)], WT[:, 3, :],
                                      start=False, stop=False)
                            ins = pe.matmul(dst, ident[0:LC, 0:LC], HR[p][:, r, :], start=False, stop=r == R - 1)
                        ins.then_inc(proj_done, 1)
                    if t == 23 and s.runs(2):
                        g = s.group(2)
                        pe.wait_ge(xn2_made, R * g + R)
                        if s.runs(0):
                            pe.wait_ge(v_copied, s.group(0) + 1)
                        for r in range(R):
                            ins = pe.transpose(pA[:, chunk(r // 2, r % 2)], xn2[s.parity(2)][:, r, :],
                                               ident[0:LC, 0:LC])
                        ins.then_inc(xn2T_done, 1)
                    if t == 0 and s.runs(3):
                        g = s.group(3)
                        pe.wait_ge(h1_copied, g + 1)
                        pe.wait_ge(xn2T_copied, g + 1)
                        for r in range(R):
                            ins = pe.matmul(pO[0:LC, r * NX:r * NX + NX],
                                            xn2T[:, r // 2, LC * (r % 2):LC * (r % 2 + 1)], gw[:, :],
                                            start=True, stop=True)
                        ins.then_inc(logit_done, 1)

                    if t == 6 and s.runs(3):
                        g = s.group(3)
                        pe.wait_ge(aff_made, g + 1)
                        pe.wait_ge(lsh_made, g + 1)
                        for c in range(2):
                            ins = pe.transpose(pO[0:G * NX, LC * c:LC * c + LC],
                                               aff[:, c, :, :].rearrange("p i e -> p (i e)"), ident[0:LC, 0:LC])
                        ins.then_inc(affT_done, 1)
                    if t == 12 and s.runs(3):
                        g = s.group(3)
                        settle(pe, g + 1, G * g)
                        pe.wait_ge(routed, g + 1)
                        pe.wait_ge(xs_copied, past(G * g))
                        for v in range(2):
                            ins = pe.transpose(pD[1][0:CAP, G * NX * v:G * NX * (v + 1)], route[:, v, :],
                                               ident[0:G * NX, 0:G * NX])
                        ins.then_inc(routeT_done, 1)
                    if t == 14 and s.runs(3):
                        g = s.group(3)
                        pe.wait_ge(routeT_copied, g + 1)
                        pe.wait_ge(y_copied, past(g))
                        for j in range(EPC):
                            ins = pe.matmul(pD[0][0:SC, 0:2 * G * NSC], slot_sel[:, j, :],
                                            routeT[:, :, :, :, j].rearrange("p v i c -> p (v i c)"),
                                            start=j == 0, stop=j == EPC - 1)
                        ins.then_inc(slot_done, 1)
                    if t in (14, 15) and s.runs(3):
                        g, i = s.group(3), t - 14
                        pe.wait_ge(spread_made, g + 1)
                        if i == 1:
                            pe.wait_ge(slot_copied, g + 1)
                        pe.matmul(pD[1 - i][0:LC, 0:SLOTS], img_sel[:, i, :], spread[:, :, :].rearrange("p e k -> p (e k)"),
                                  start=True, stop=True).then_inc(bc_done, 1)
                    if t in (17, 19) and s.runs(3):
                        g, i = s.group(3), t // 2 - 8
                        pe.wait_ge(hotG_made, 2 * (G * g + i + 1))
                        for c in range(2):
                            ins = pe.matmul(pD[1 - i][:, 0:SLOTS], xn2[s.parity(3)][:, 2 * i + c, :], hotG[:, 2 * i + c, :],
                                            start=c == 0, stop=c == 1)
                        ins.then_inc(xg_done, 1)
                    if t >= 21 and s.runs(3):
                        g, a, part = s.group(3), (t - 21) // 2, (t - 21) % 2
                        if a == 0:
                            pe.wait_ge(xg_copied, G * (g + 1))
                        experts(0, a, part, XG, m1_done)
                    if t < 4 and s.runs(4):
                        g, a, part = s.group(4), t // 2, t % 2
                        pe.wait_ge(gelu_made, 2 * g + a + 1)
                        experts(1, a, part, HID, m2_done)
                    if t == 6 and s.runs(4):
                        g = s.group(4)
                        pe.wait_ge(xe_copied, 2 * (g + 1))
                        for i in range(G):
                            for c in range(NSC):
                                ins = pe.transpose(pD[i][0:SC, D * c:D * c + D],
                                                   XE[:, i, EPC * c:EPC * (c + 1), :].rearrange("p e k -> p (e k)"),
                                                   ident[:, :])
                            ins.then_inc(xs_done, 1)
                    if t in (8, 9, 10, 11) and s.runs(4):
                        g, r = s.group(4), t - 8
                        i, c = divmod(r, 2)
                        pe.wait_ge(xs_copied, G * g + G)
                        pe.wait_ge(hotS_made, G * NSC * (g + 1))
                        dst = pD[0][0:LC, r * D:r * D + D]
                        pe.matmul(dst, ident[0:LC, 0:LC], H1[s.parity(4)][:, r, :], start=True, stop=False)
                        for n in range(NSC):
                            ins = pe.matmul(dst, hotS[:, i, n, LC * c:LC * c + LC], XS[:, i, n, :],
                                            start=False, stop=n == NSC - 1)
                        if r == R - 1:
                            ins.then_inc(y_done, 1)

                    if m.valid:
                        pe.wait_ge(prob_made, m.n + 1)
                        if m.pair_starts:
                            pe.wait_ge(pt_copied, past(m.pairs - 1))
                        for c in range(2):
                            at = 256 * m.side + 128 * c
                            ins = pe.transpose(pT[m.bank][0:LC, at:at + 128], prob[:, m.buf, LC * c:LC * c + LC],
                                               ident[:, :])
                        ins.then_inc(pt_done, 1)

            all_steps(body, pe)


_INS = ['x', 'cls_tok', 'L0_tok_W', 'L0_tok_b', 'L0_tok_token', 'L0_tok_pos', 'L0_attn_Wq', 'L0_attn_bq',
        'L0_attn_Wk', 'L0_attn_bk', 'L0_attn_Wv', 'L0_attn_bv', 'L0_attn_Wo', 'L0_attn_bo',
        'L0_ffn_gate_weight', 'L0_ffn_w1', 'L0_ffn_b1', 'L0_ffn_w2', 'L0_ffn_b2']
_OUT = (64, 198, 128)


def kernel(**inputs):
    import numpy as _np
    import concourse.bacc as _bacc
    from concourse import mybir as _mybir
    from concourse.bass_utils import run_bass_kernel_spmd as _run

    nc = _bacc.Bacc("TRN2", target_bir_lowering=False, num_devices=1)
    arrays, args = {}, []
    for name in _INS:
        a = _np.ascontiguousarray(inputs[name])
        arrays[f"in_{name}_dram"] = a
        args.append(nc.dram_tensor(f"in_{name}_dram", a.shape, _mybir.dt.from_np(a.dtype), kind="ExternalInput").ap())
    out = nc.dram_tensor("out_dram", _OUT, _mybir.dt.float32, kind="ExternalOutput").ap()
    vit_block(nc, *args, out)
    r = _run(nc, [arrays], core_ids=[0])
    return r.results[0]["out_dram"]
```

```python
import concourse.bass as bass
from concourse import mybir
from contextlib import ExitStack



def vit_block(nc, x, cls_tok, tok_W, tok_b, tok_token, tok_pos, Wq, bq, Wk, bk, Wv, bv, Wo, bo,
              gate_weight, w1, b1, w2, b2, out):
    f32 = mybir.dt.float32
    bf16 = mybir.dt.bfloat16
    u32 = mybir.dt.uint32
    ALU = mybir.AluOpType
    ACT = mybir.ActivationFunctionType
    AX = mybir.AxisListType

    B, C, IMG, _ = x.shape
    D = tok_W.shape[0]
    P = 14
    NP = IMG // P
    L = NP * NP + 2
    LC = L // 2
    H = 8
    E = D // H
    NX = gate_weight.shape[1]
    KEEP = 26
    CAP = L // NX * 2
    SLOTS = NX * CAP
    EPC = 4
    NSC = NX // EPC
    SC = EPC * CAP
    G = 2
    NG = B // G
    R = G * 2
    SH = 3
    CP = C * P
    QS = -(-P // SH)
    XPAD = 2 * P
    NEG = -3.4028234663852886e38
    EPS = 1e-5
    EXP_LN_TABLES = "natural_log_exp_and_others"

    TILES = [("tail", 0, 0)]
    for i in range(G):
        TILES += [("full", i, h) for h in range(H)]
        TILES += [("half", i, h) for h in range(0, H, 2)]
    T = len(TILES)
    PAIRS = T // 2 + 1
    NT = T * NG
    TAILR = 64 // H
    EMBED = (4, 4, 3, 3, 3, 3, 2, 2)
    NB = 5
    PE_LAG = 6
    HOT_SLOTS = (15, 17, 20, 22, 24)
    HOT_DVE = 1
    EV_LAG = 6
    assert L == 198 and T == 25 and T % NB == 0 and G * H * TAILR == 128

    with ExitStack() as ctx:
        def sb(name, shape, dt=f32):
            return ctx.enter_context(nc.sbuf_tensor(name, shape, dt))

        def ps(name, shape):
            return ctx.enter_context(nc.psum_tensor(name, shape, f32))

        def sem(name):
            return ctx.enter_context(nc.semaphore(name))

        def sb2(name, shape, dt=f32):
            return [sb(f"{name}{p}", shape, dt) for p in range(2)]

        ident = sb("ident", [128, 128])
        ones3 = sb("ones3", [96, LC], bf16)
        tokWT = sb("tokWT", [SH * CP, QS, D])
        posb = sb("posb", [LC, 2, D])
        WT = sb("WT", [D, 4, D])
        bcol = sb("bcol", [D, 3])
        bq4 = sb("bq4", [D, 1])
        bias3 = sb("bias3", [96, 3, D], bf16)
        exp_sel = sb("exp_sel", [96, NX], bf16)
        gw = sb("gw", [D, NX])
        w1s = sb("w1s", [D, NX, D])
        w2s = sb("w2s", [D, NX, D])
        img_sel = sb("img_sel", [G * NX, G, LC], bf16)
        own_exp = sb("own_exp", [G * NX, NX])
        slot_sel = sb("slot_sel", [CAP, EPC, SC])
        tok_iota = sb("tok_iota", [SC, L])
        minus_tok = sb("minus_tok", [LC, 2])
        one_col = sb("one_col", [LC, 1])
        eps_col = sb("eps_col", [LC, 1])

        X = sb("X", [SH * CP, G, XPAD + NP * IMG])
        Hs = sb("Hs", [LC, R, D])
        xn = sb("xn", [LC, R, D])
        xnT = sb("xnT", [D, G, L])
        QT = sb("QT", [D, G, L])
        QM = sb2("QM", [D, G, H, L])
        QMtail = sb2("QMtail", [D, G, H * TAILR])
        own_head = sb("own_head", [D, H])
        KT = sb2("KT", [D, G, L])
        VP = sb2("VP", [LC, R, H, 2 * E])
        stats = sb("stats", [LC, R, 6])
        mv = sb("mv", [LC, R, 2])
        rstd = sb("rstd", [LC, 5, R])
        top = sb("top", [128, NB, 7 * 8])
        left = sb("left", [128, NB, L])
        ex = sb("ex", [128, NB, L])
        nmax = sb("nmax", [128, NB])
        extop = sb("extop", [128, KEEP])
        rsum = sb("rsum", [128, NB])
        rinv = sb("rinv", [128, NB])
        prob = sb("prob", [128, NB, L])
        PT = [sb(f"PT{p}", [128, G, 2, H, L]) for p in range(2)]
        setup_room = PT[1][:, 0, :, :, :].rearrange("p c h l -> p (c h l)")
        wload = setup_room[:, 0:C * P * P]
        wraw = setup_room[:, 768:768 + 4 * D].rearrange("p (n d) -> p n d", n=4)
        wsort = setup_room[:, 1792:1792 + C * P * P]
        biasr = setup_room[0:LC, 1536:1536 + 2 * D].rearrange("p (c d) -> p c d", c=2)
        braw = setup_room[0:96, 2560:2560 + 3 * D].rearrange("p (n d) -> p n d", n=3)
        setup_room2 = PT[1][:, 1, :, :, :].rearrange("p c h l -> p (c h l)")
        brest = setup_room2[0:96, 0:3 * D].rearrange("p (n d) -> p n d", n=3)
        bpart = sb("bpart", [96, 3, D], bf16)
        HR = sb2("HR", [LC, R, D])
        OT = sb("OT", [D, G, L])
        H1 = sb2("H1", [LC, R, D])
        xn2 = sb2("xn2", [LC, R, D])
        xn2T = sb("xn2T", [D, G, L])
        stats2 = sb("stats2", [LC, R, 6])
        mv2 = sb("mv2", [LC, R, 2])
        rstd2 = sb("rstd2", [LC, 5, R])
        lmax = sb("lmax", [LC, R])
        lsh = sb("lsh", [LC, R, NX])
        lex = sb("lex", [LC, R, NX])
        lsum = sb("lsum", [LC, R])
        linv = sb("linv", [LC, R])
        aff = sb("aff", [LC, 2, G, NX])
        affT = sb("affT", [G * NX, 3, L])
        route = sb("route", [G * NX, 2, CAP])
        idxu = sb("idxu", [G * NX, CAP], u32)
        routeT = sb("routeT", [CAP, 2, G, NSC, EPC])
        spread = sb("spread", [G * NX, NX, CAP], bf16)
        slotv = sb("slotv", [SC, 2, G, NSC])
        hotG = sb("hotG", [LC, R, SLOTS])
        hotS = sb("hotS", [SC, G, NSC, L])
        XG = sb("XG", [D, NX, G, CAP])
        HID = sb("HID", [D, NX, G * CAP])
        XE = XG[:, :, :, :].rearrange("p e i k -> p (e i k)").rearrange("p (i e k) -> p i e k", i=G, e=NX)
        XS = hotG[0:SC, :, :].rearrange("p r s -> p (r s)")[:, 0:G * NSC * D] \
            .rearrange("p (i c d) -> p i c d", i=G, c=NSC)
        Y = sb("Y", [LC, R, D])

        pS = [ps(f"pS{p}", [128, 512]) for p in range(2)]
        pT = [ps(f"pT{p}", [128, 512]) for p in range(2)]
        pO = ps("pO", [128, 512])
        pA = ps("pA", [128, 512])
        pD = [ps(f"pD{p}", [128, 512]) for p in range(2)]

        w_raw = sem("w_raw")
        w_loaded = sem("w_loaded")
        experts_loaded = sem("experts_loaded")
        ident_ready = sem("ident_ready")
        const_step = sem("const_step")
        zero_ready = sem("zero_ready")
        wsorted = sem("wsorted")
        bias_split = sem("bias_split")
        exp_sel_step = sem("exp_sel_step")
        own_head_step = sem("own_head_step")
        tail_made = sem("tail_made")
        wt_done = sem("wt_done")
        wt_copied = sem("wt_copied")
        posb_ready = sem("posb_ready")
        bq4_ready = sem("bq4_ready")
        x_loaded = sem("x_loaded")
        q_spread = [sem(f"q_spread{p}") for p in range(2)]
        hr_copied = sem("hr_copied")
        stored = sem("stored")
        embedded = sem("embedded")
        h_copied = sem("h_copied")
        stat_step = sem("stat_step")
        var_exp = sem("var_exp")
        newton = sem("newton")
        xn_made = sem("xn_made")
        xnT_done = sem("xnT_done")
        xnT_copied = sem("xnT_copied")
        q_done = sem("q_done")
        q_copied = sem("q_copied")
        k_done = sem("k_done")
        k_copied = sem("k_copied")
        v_done = sem("v_done")
        v_copied = sem("v_copied")
        scored = sem("scored")
        top_found = [sem(f"top_found{r}") for r in range(4)]
        taken = [sem(f"taken{r}") for r in range(4)]
        nmax_made = sem("nmax_made")
        exp_made = sem("exp_made")
        sum_made = sem("sum_made")
        inv_made = sem("inv_made")
        kept_made = sem("kept_made")
        prob_made = sem("prob_made")
        pt_done = sem("pt_done")
        pt_copied = sem("pt_copied")
        pv_done = sem("pv_done")
        o_copied = sem("o_copied")
        proj_done = sem("proj_done")
        h1_copied = sem("h1_copied")
        stat2_step = sem("stat2_step")
        var2_exp = sem("var2_exp")
        newton2 = sem("newton2")
        xn2_made = sem("xn2_made")
        xn2T_done = sem("xn2T_done")
        xn2T_copied = sem("xn2T_copied")
        logit_done = sem("logit_done")
        lmax_made = sem("lmax_made")
        lsh_made = sem("lsh_made")
        lex_made = sem("lex_made")
        lsum_made = sem("lsum_made")
        linv_made = sem("linv_made")
        aff_made = sem("aff_made")
        affT_done = sem("affT_done")
        affT_copied = sem("affT_copied")
        route_step = sem("route_step")
        routed = sem("routed")
        routeT_done = sem("routeT_done")
        routeT_copied = sem("routeT_copied")
        spread_made = sem("spread_made")
        slot_done = sem("slot_done")
        slot_copied = sem("slot_copied")
        bc_done = sem("bc_done")
        far_made = sem("far_made")
        hotG_made = sem("hotG_made")
        hotS_first = sem("hotS_first")
        hotS_made = sem("hotS_made")
        xg_done = sem("xg_done")
        xg_copied = sem("xg_copied")
        m1_done = sem("m1_done")
        gelu_made = sem("gelu_made")
        m2_done = sem("m2_done")
        xe_copied = sem("xe_copied")
        xs_done = sem("xs_done")
        xs_copied = sem("xs_copied")
        y_done = sem("y_done")
        y_copied = sem("y_copied")

        N_W_LOADS = 18

        class Step:

            def __init__(self, half, par):
                self.half, self.par = half, par
                self.k = 2 * half + par

            def known(self):
                return isinstance(self.half, int)

            def runs(self, lag):
                return not self.known() or 0 <= self.k - lag < NG

            def group(self, lag):
                return self.k - lag

            def parity(self, lag):
                return (self.par - lag) % 2

            def rounds(self, lag):
                p = self.parity(lag)
                return self.half + (self.par - lag - p) // 2

            def tile(self, t):
                return Tile(self, t)

        class Tile:
            def __init__(self, step, t):
                back = t < 0
                self.n = (step.k - 1) * T + t
                self.valid = not step.known() or 0 <= self.n < NT
                self.par = ((step.par - 1) * T + t) % 2
                self.buf = t % NB
                self.gpar = step.parity(2 if back else 1)
                self.group = step.k - (2 if back else 1)
                self.t = t % T
                self.kind, self.img, self.head = TILES[self.t]
                pair = (self.t + 1) // 2
                self.pairs = self.group * PAIRS + pair
                self.bank = (self.gpar + pair) % 2
                self.side = (self.t + 1) % 2 if self.t else 0
                self.pair_starts = self.t == 0 or self.t % 2 == 1
                self.pair_ends = self.t % 2 == 0

        def past(count):
            return max(count, 0) if isinstance(count, int) else count

        def settle(eng, *values):
            for v in values:
                if not isinstance(v, int):
                    eng.compute_val(v)
            eng.wait_ge(const_step, 1)

        def all_steps(body, eng):
            for k in range(6):
                body(Step(k // 2, k % 2))
            with eng.Fori(3, NG // 2 - 1) as half:
                body(Step(half, 0))
                body(Step(half, 1))
            for k in range(NG - 2, NG + 4):
                body(Step(k // 2, k % 2))

        block = ctx.enter_context(nc.Block())

        @block.sync
        def _(sp):
            def load_x(s):
                g = s.group(-1)
                sp.wait_ge(embedded, past(g))
                for i in range(G):
                    for sh in range(SH):
                        for c in range(C):
                            src = x[G * g + i, c].rearrange("(n p) w -> p n w", p=P)[:, :, sh:IMG] \
                                if s.known() else \
                                x[bass.ds(G * g + i, 1), c].rearrange("a (n p) w -> (a p) n w", p=P)[:, :, sh:IMG]
                            lo = (sh * C + c) * P
                            dst = X[lo:lo + P, i, XPAD:].rearrange("p (n w) -> p n w", n=NP)
                            sp.dma_start(dst[:, :, 0:IMG - sh], src).then_inc(x_loaded, 16)

            sp.dma_start(wload[:, :], tok_W[:, :]).then_inc(w_raw, 16)
            for n, w in enumerate((Wq, Wk, Wv, Wo)):
                sp.dma_start(wraw[:, n, :], w[:, :]).then_inc(w_raw, 16)
            sp.wait_ge(zero_ready, 2)
            load_x(Step(-1, 1))
            for n, v in enumerate((bq, bk, bv)):
                sp.dma_start(bcol[:, n:n + 1], v.rearrange("(p a) -> p a", a=1)).then_inc(w_loaded, 16)
            brow = tok_b.rearrange("(a n) -> a n", a=1)
            sp.dma_start(posb[1:LC, 0, :], tok_pos[0:LC - 1, :]).then_inc(w_loaded, 16)
            sp.dma_start(posb[:, 1, :], tok_pos[LC - 1:L - 1, :]).then_inc(w_loaded, 16)
            sp.dma_start(biasr[0:1, 0, :], cls_tok[0, :, :]).then_inc(w_loaded, 16)
            sp.dma_start(biasr[1:2, 0, :], tok_token[:, :]).then_inc(w_loaded, 16)
            sp.dma_start(biasr[2:LC, 0, :], brow.broadcast_to([LC - 2, D])).then_inc(w_loaded, 16)
            sp.dma_start(biasr[:, 1, :], brow.broadcast_to([LC, D])).then_inc(w_loaded, 16)
            for part in range(3):
                sp.dma_start(braw[32 * part:32 * part + NX, 0, :], b1[:, :]).then_inc(w_loaded, 16)
                sp.dma_start(braw[32 * part:32 * part + NX, 1, :], b2[:, :]).then_inc(w_loaded, 16)
                sp.dma_start(braw[32 * part:32 * part + 1, 2, :], bo.rearrange("(a n) -> a n", a=1)).then_inc(w_loaded, 16)
            sp.dma_start(gw[:, :], gate_weight[:, :]).then_inc(experts_loaded, 16)
            sp.dma_start(w1s[:, :, :], w1.rearrange("e d f -> d e f")).then_inc(experts_loaded, 16)
            sp.dma_start(w2s[:, :, :], w2.rearrange("e f d -> f e d")).then_inc(experts_loaded, 16)

            def body(s):
                if s.runs(1):
                    p = s.parity(1)
                    settle(sp, s.group(1) + 1, s.group(1) - 1)
                    sp.wait_ge(h_copied, s.group(1) + 1)
                    sp.wait_ge(proj_done, past(s.group(1) - 1))
                    sp.dma_start(HR[p][:, :, :], Hs[:, :, :]).then_inc(hr_copied, 16)
                if s.runs(-1):
                    load_x(s)
                if s.runs(0):
                    p = s.parity(0)
                    settle(sp, s.group(0) + 1, (s.group(0) - 1) * T)
                    sp.wait_ge(q_copied, s.group(0) + 1)
                    sp.wait_ge(scored, past((s.group(0) - 1) * T))
                    for h in range(H):
                        rows = slice(h * E, h * E + E)
                        sp.dma_start(QM[p][rows, :, h, :], QT[rows, :, :]).then_inc(q_spread[p], 16)
                if s.runs(4):
                    g = s.group(4)
                    sp.wait_ge(y_copied, g + 1)
                    dst = out[G * g:G * g + G] if s.known() else out[bass.ds(G * g, G)]
                    sp.dma_start(dst.rearrange("b (c p) d -> p b c d", p=LC),
                                 Y[:, :, :].rearrange("p (b c) d -> p b c d", b=G)) \
                      .then_inc(stored, 16)

            all_steps(body, sp)
            sp.wait_ge(stored, 16 * NG)

        @block.gpsimd
        def _(pool):
            pool.memset(X[:, :, 0:XPAD], 0.0)
            pool.memset(ident[:, :], 0.0).then_inc(const_step, 1)
            pool.memset(braw[:, :, :], 0.0)
            pool.memset(posb[:, :, :], 0.0).then_inc(zero_ready, 2)
            pool.wait_ge(const_step, 1)
            pool.affine_select(out=ident[:, :], in_=ident[:, :], compare_op=ALU.not_equal, fill=1.0,
                               base=0, pattern=[[-1, 128]], channel_multiplier=1).then_inc(ident_ready, 1)
            for p in range(2):
                pool.memset(VP[p][:, :, :, :], 0.0)
                pool.memset(QM[p][:, :, :, :], 0.0).then_inc(zero_ready, 1)
            pool.memset(ones3[:, :], 1.0)
            pool.memset(exp_sel[:, :], 0.0)
            pool.memset(own_head[:, :], 1.0)
            pool.memset(eps_col[:, :], EPS)
            pool.memset(one_col[:, :], 1.0)
            pool.memset(img_sel[:, :, :], 1.0)
            pool.memset(own_exp[:, :], 0.0)
            pool.memset(slot_sel[:, :, :], 0.0)
            pool.memset(top[:, :, :], NEG)
            pool.iota(tok_iota[:, :], pattern=[[1, L]], base=0, channel_multiplier=0,
                      allow_small_or_imprecise_dtypes=True)
            pool.iota(minus_tok[:, :], pattern=[[-LC, 2]], base=0, channel_multiplier=-1,
                      allow_small_or_imprecise_dtypes=True).then_inc(const_step, 1)
            pool.wait_ge(const_step, 2)
            for i in range(G):
                pool.affine_select(out=own_exp[:, :], in_=own_exp[:, :], compare_op=ALU.not_equal, fill=1.0,
                                   base=-NX * i, pattern=[[-1, NX]], channel_multiplier=1) \
                    .then_inc(const_step, 1)
                pool.wait_ge(const_step, 3 + i)
            pool.affine_select(out=own_head[:, :], in_=own_head[:, :], compare_op=ALU.is_ge, fill=0.0,
                               base=0, pattern=[[-E, H]], channel_multiplier=1).then_inc(own_head_step, 1)
            pool.wait_ge(own_head_step, 1)
            pool.affine_select(out=own_head[:, :], in_=own_head[:, :], compare_op=ALU.is_ge, fill=0.0,
                               base=E - 1, pattern=[[E, H]], channel_multiplier=-1).then_inc(own_head_step, 1)
            for part in range(3):
                pool.affine_select(out=exp_sel[:, :], in_=exp_sel[:, :], compare_op=ALU.not_equal, fill=1.0,
                                   base=-32 * part, pattern=[[-1, NX]], channel_multiplier=1) \
                    .then_inc(exp_sel_step, 1)
                pool.wait_ge(exp_sel_step, part + 1)
            pool.affine_select(out=slot_sel[:, :, :], in_=slot_sel[:, :, :], compare_op=ALU.not_equal, fill=1.0,
                               base=0, pattern=[[CAP, EPC], [-1, SC]], channel_multiplier=1)
            pool.affine_select(out=img_sel[:, :, :], in_=img_sel[:, :, :], compare_op=ALU.is_ge, fill=0.0,
                               base=0, pattern=[[-NX, G], [0, LC]], channel_multiplier=1) \
                .then_inc(const_step, 1)
            pool.wait_ge(const_step, 3 + G)
            pool.affine_select(out=img_sel[:, :, :], in_=img_sel[:, :, :], compare_op=ALU.is_ge, fill=0.0,
                               base=NX - 1, pattern=[[NX, G], [0, LC]], channel_multiplier=-1) \
                .then_inc(const_step, 1)

            def refine(mvt, r, exped, done, n):
                var = mvt[:, :, 1]
                settle(pool, 2 * n + 2)
                pool.wait_ge(exped, 2 * n + 2)
                pool.tensor_tensor(r[:, 4, :], r[:, 1, :], r[:, 1, :], ALU.mult).then_inc(done, 1)
                pool.tensor_scalar(r[:, 0, :], var, EPS, -0.5, ALU.add, ALU.mult).then_inc(done, 1)
                pool.wait_ge(done, 7 * n + 2)
                pool.tensor_tensor(r[:, 4, :], r[:, 4, :], r[:, 0, :], ALU.mult).then_inc(done, 1)
                settle(pool, 7 * n + 3)
                pool.wait_ge(done, 7 * n + 3)
                pool.tensor_scalar(r[:, 4, :], r[:, 4, :], 1.5, None, ALU.add).then_inc(done, 1)
                pool.wait_ge(done, 7 * n + 4)
                pool.tensor_tensor(r[:, 2, :], r[:, 4, :], r[:, 1, :], ALU.mult).then_inc(done, 1)
                pool.wait_ge(done, 7 * n + 5)
                pool.tensor_tensor(r[:, 3, :], mvt[:, :, 0], r[:, 2, :], ALU.mult).then_inc(done, 1)
                settle(pool, 7 * n + 6)
                pool.wait_ge(done, 7 * n + 6)
                pool.tensor_scalar(r[:, 3, :], r[:, 3, :], -1.0, None, ALU.mult).then_inc(done, 1)

            def body(s):
                for t in range(T):
                    if t == 11 and s.runs(0):
                        refine(mv, rstd, var_exp, newton, s.group(0))
                    if t == 19 and s.runs(0):
                        p, g = s.parity(0), s.group(0)
                        if s.known() and g == 0:
                            pool.wait_ge(own_head_step, 2)
                        pool.wait_ge(q_copied, g + 1)
                        pool.wait_ge(scored, past((g - 1) * T))
                        pool.tensor_tensor(QMtail[p][:, :, :].rearrange("p i (h r) -> p i h r", h=H),
                                           QT[:, :, L - TAILR:L].rearrange("p i (a r) -> p i a r", a=1)
                                           .broadcast_to([D, G, H, TAILR]),
                                           own_head[:, :].rearrange("p (a h b) -> p a h b", a=1, b=1)
                                           .broadcast_to([D, G, H, TAILR]), ALU.mult).then_inc(tail_made, 1)
                    if t == 18 and s.runs(2):
                        refine(mv2, rstd2, var2_exp, newton2, s.group(2))
                    if t == 4 and s.runs(3):
                        g = s.group(3)
                        pool.wait_ge(linv_made, g + 1)
                        pool.wait_ge(affT_done, past(g))
                        pool.tensor_tensor(aff[:, :, :, :].rearrange("p c i e -> p i c e"),
                                           lex[:, :, :].rearrange("p (i c) e -> p i c e", i=G),
                                           linv[:, :].rearrange("p (i c a) -> p i c a", i=G, a=1)
                                           .broadcast_to([LC, G, 2, NX]), ALU.mult).then_inc(aff_made, 1)
                    if t == 11 and s.runs(3):
                        g = s.group(3)
                        pool.wait_ge(routed, g + 1)
                        pool.wait_ge(bc_done, past(G * g))
                        pool.tensor_tensor(spread[:, :, :],
                                           route[:, 0:1, :].broadcast_to([G * NX, NX, CAP]),
                                           own_exp[:, :].rearrange("p (e a) -> p e a", a=1)
                                           .broadcast_to([G * NX, NX, CAP]), ALU.mult).then_inc(spread_made, 1)
                    late = t in (0, 2)
                    if (late and s.runs(4)) or (t in HOT_SLOTS and s.runs(3)):
                        g = s.group(4 if late else 3)
                        n = G * NSC - 2 + t // 2 if late else HOT_DVE + HOT_SLOTS.index(t)
                        i, c = divmod(n, NSC)
                        settle(pool, g + 1, g)
                        pool.wait_ge(slot_copied, g + 1)
                        pool.wait_ge(y_done, past(g))
                        pool.tensor_scalar(hotS[:, i, c, :], tok_iota[:, :], slotv[:, 0, i, c:c + 1],
                                           slotv[:, 1, i, c:c + 1], ALU.is_equal, ALU.mult).then_inc(hotS_made, 1)
                    q = s.tile(t - 2)
                    if q.valid:
                        settle(pool, q.n + 1, q.n - NB + 1)
                        pool.wait_ge(inv_made, q.n + 1)
                        pool.wait_ge(taken[3], q.n + 1)
                        pool.tensor_scalar(left[:, q.buf, :], left[:, q.buf, :], NEG, rinv[:, q.buf:q.buf + 1],
                                           ALU.is_equal, ALU.mult).then_inc(kept_made, 1)
                        pool.wait_ge(kept_made, q.n + 1)
                        pool.wait_ge(exp_made, q.n + 1)
                        pool.wait_ge(pt_done, past(q.n - NB + 1))
                        pool.tensor_tensor(prob[:, q.buf, :], left[:, q.buf, :], ex[:, q.buf, :], ALU.mult) \
                            .then_inc(prob_made, 1)

            all_steps(body, pool)

        @block.vector
        def _(dve):
            dve.wait_ge(w_loaded, 16 * N_W_LOADS)
            dve.wait_ge(zero_ready, 2)
            dve.tensor_tensor(posb[:, :, :], posb[:, :, :], biasr[:, :, :], ALU.add).then_inc(posb_ready, 1)
            dve.tensor_copy(bpart[:, :, :], braw[:, :, :]).then_inc(bias_split, 1)
            dve.wait_ge(bias_split, 1)
            dve.tensor_copy(bias3[0:32, :, :], bpart[0:32, :, :]).then_inc(bias_split, 1)
            dve.tensor_tensor(brest[:, :, :], braw[:, :, :], bpart[:, :, :], ALU.subtract).then_inc(bias_split, 1)
            dve.wait_ge(bias_split, 3)
            dve.tensor_copy(bpart[:, :, :], brest[:, :, :]).then_inc(bias_split, 1)
            dve.wait_ge(bias_split, 4)
            dve.tensor_copy(bias3[32:64, :, :], bpart[32:64, :, :]).then_inc(bias_split, 1)
            dve.tensor_tensor(brest[:, :, :], brest[:, :, :], bpart[:, :, :], ALU.subtract).then_inc(bias_split, 1)
            dve.wait_ge(bias_split, 6)
            dve.tensor_copy(bias3[64:96, :, :], brest[64:96, :, :]).then_inc(bias_split, 1)
            dve.wait_ge(const_step, 4 + G)

            def found(q, r):
                settle(dve, q.n + 1, q.n - NB + 1)
                if r == 0:
                    dve.wait_ge(scored, q.n + 1)
                    dve.wait_ge(inv_made, past(q.n - NB + 1))
                else:
                    dve.wait_ge(taken[r - 1], q.n + 1)
                src = pS[q.par][:, 0:L] if r == 0 else left[:, q.buf, :]
                dve.max(top[:, q.buf, 8 * r:8 * r + 8], src).then_inc(top_found[r], 1)

            def take(q, r):
                settle(dve, q.n + 1, q.n - NB + 1)
                dve.wait_ge(top_found[r], q.n + 1)
                if r == 0:
                    dve.wait_ge(prob_made, past(q.n - NB + 1))
                src = pS[q.par][:, 0:L] if r == 0 else left[:, q.buf, :]
                what = top[:, q.buf, 8 * r:8 * r + 8]
                if r == 3:
                    what = top[:, q.buf, 24:56].rearrange("p (a b) -> p a b", b=8)[:, :, 0:2]
                dve.match_replace(left[:, q.buf, :], what, src, NEG).then_inc(taken[r], 1)

            def layer_stats(src, ready, st, mvt, step, refined, n):
                dve.wait_ge(ready, n + 1)
                dve.wait_ge(refined, past(7 * n))
                for r in range(R):
                    dve.bn_stats(st[:, r, :], src[:, r, :]).then_inc(step, 1)

            def layer_moments(st, mvt, step, n):
                settle(dve, 2 * R * n + R)
                dve.wait_ge(step, 2 * R * n + R)
                for r in range(R):
                    dve.bn_aggr(mvt[:, r, :], st[:, r, :]).then_inc(step, 1)

            def between(s, t):
                if t == 10 and s.runs(0):
                    layer_moments(stats, mv, stat_step, s.group(0))
                if t == 17 and s.runs(2):
                    layer_moments(stats2, mv2, stat2_step, s.group(2))
                if t == 2 and s.runs(3):
                    g = s.group(3)
                    dve.wait_ge(lmax_made, g + 1)
                    dve.wait_ge(lex_made, past(g))
                    dve.tensor_tensor(lsh[:, :, :], pO[0:LC, 0:R * NX].rearrange("p (r e) -> p r e", r=R),
                                      lmax[:, :].rearrange("p (r a) -> p r a", a=1).broadcast_to([LC, R, NX]),
                                      ALU.subtract).then_inc(lsh_made, 1)
                if t == 4 and s.runs(3):
                    g = s.group(3)
                    dve.wait_ge(lsum_made, g + 1)
                    dve.wait_ge(aff_made, past(g))
                    dve.reciprocal(linv[:, :], lsum[:, :]).then_inc(linv_made, 1)
                if t in (8, 9, 10) and s.runs(3):
                    g, r = s.group(3), t - 8
                    n = 8 * g + 3 * r
                    m = route[:, 1, 8 * r:8 * r + 8]
                    settle(dve, n + 1)
                    dve.wait_ge(route_step, n + 1)
                    dve.max_index(idxu[:, 8 * r:8 * r + 8], m, affT[:, r, :]).then_inc(route_step, 1)
                    if r < 2:
                        dve.match_replace(affT[:, r + 1, :], m, affT[:, r, :], NEG).then_inc(route_step, 1)

            def body(s):
                for t in range(T):
                    q, o, f = s.tile(t), s.tile(t - 1), s.tile(t - 2)
                    if q.valid:
                        found(q, 0)
                    if o.valid:
                        found(o, 2)
                    between(s, t)
                    if q.valid:
                        take(q, 0)
                    if o.valid:
                        take(o, 2)
                    if q.valid:
                        found(q, 1)
                    if o.valid:
                        found(o, 3)
                    if q.valid:
                        take(q, 1)
                    if o.valid:
                        take(o, 3)
                    if f.valid:
                        dve.wait_ge(sum_made, f.n + 1)
                        dve.wait_ge(kept_made, past(f.n - NB + 1))
                        dve.reciprocal(rinv[:, f.buf:f.buf + 1], rsum[:, f.buf:f.buf + 1]).then_inc(inv_made, 1)

                    if t == 9 and s.runs(0):
                        layer_stats(Hs, h_copied, stats, mv, stat_step, newton, s.group(0))
                    if t == 16 and s.runs(2):
                        layer_stats(H1[s.parity(2)], h1_copied, stats2, mv2, stat2_step, newton2, s.group(2))
                    if t == 1 and s.runs(3):
                        g = s.group(3)
                        lg = pO[0:LC, 0:R * NX].rearrange("p (r e) -> p r e", r=R)
                        dve.wait_ge(logit_done, g + 1)
                        dve.tensor_reduce(lmax[:, :], lg, axis=AX.X, op=ALU.max).then_inc(lmax_made, 1)
                    if t == 3 and s.runs(3):
                        g = s.group(3)
                        dve.wait_ge(lex_made, g + 1)
                        dve.tensor_reduce(lsum[:, :], lex[:, :, :], axis=AX.X, op=ALU.add).then_inc(lsum_made, 1)
                    if t in (7, 8, 9) and s.runs(3):
                        g, r = s.group(3), t - 7
                        n = 8 * g + 3 * r
                        settle(dve, g + 1, g, n)
                        if r == 0:
                            dve.wait_ge(affT_copied, g + 1)
                            dve.wait_ge(spread_made, past(g))
                            dve.wait_ge(routeT_done, past(g))
                        else:
                            dve.wait_ge(route_step, past(n))
                        dve.max(route[:, 1, 8 * r:8 * r + 8], affT[:, r, :]).then_inc(route_step, 1)
                    if t == 10 and s.runs(3):
                        g = s.group(3)
                        dve.wait_ge(route_step, 8 * g + 8)
                        dve.tensor_copy(route[:, 0, :], idxu[:, :]).then_inc(routed, 1)
                    if t == 17 and s.runs(3):
                        g, n = s.group(3), 0
                        dve.wait_ge(slot_copied, g + 1)
                        dve.wait_ge(y_done, past(g))
                        dve.tensor_scalar(hotS[:, n // NSC, n % NSC, :], tok_iota[:, :], slotv[:, 0, n // NSC, n % NSC:n % NSC + 1],
                                          slotv[:, 1, n // NSC, n % NSC:n % NSC + 1], ALU.is_equal, ALU.mult) \
                           .then_inc(hotS_first, 1)

            all_steps(body, dve)

        @block.scalar
        def _(act):
            act.preload_act_table_set(EXP_LN_TABLES)
            act.wait_ge(w_raw, 16 * 5)
            act.activation(wsort.rearrange("d (q c) -> d q c", q=P), wload.rearrange("d (c q) -> d q c", q=P),
                           ACT.Copy).then_inc(wsorted, 1)
            for n in range(QS + 4):
                act.wait_ge(wt_done, n + 1)
                if n < QS:
                    rows = min(SH, P - SH * n) * CP
                    act.activation(tokWT[0:rows, n, :], pT[n % 2][0:rows, 0:D], ACT.Copy).then_inc(wt_copied, 1)
                else:
                    act.activation(WT[:, n - QS, :], pT[n % 2][:, 0:D], ACT.Copy).then_inc(wt_copied, 1)
            act.wait_ge(w_loaded, 16 * N_W_LOADS)
            act.activation(bq4[:, :], bcol[:, 0:1], ACT.Copy, scale=0.25).then_inc(bq4_ready, 1)
            act.wait_ge(bq4_ready, 1)
            act.wait_ge(const_step, 4 + G)

            def inv_std(mvt, r, step, exped, refined, n):
                act.wait_ge(step, past(2 * R * n + 2 * R))
                act.wait_ge(refined, past(7 * n))
                act.activation(r[:, 0, :], mvt[:, :, 1], ACT.Ln, bias=eps_col[:, 0:1]).then_inc(exped, 1)
                act.wait_ge(exped, 2 * n + 1)
                act.activation(r[:, 1, :], r[:, 0, :], ACT.Exp, scale=-0.5).then_inc(exped, 1)

            def body(s):
                for t in range(T):
                    q, o, m = s.tile(t), s.tile(t - 1), s.tile(t - EV_LAG)
                    if q.valid:
                        act.wait_ge(top_found[0], q.n + 1)
                        act.wait_ge(sum_made, past(q.n - NB + 1))
                        act.activation(nmax[:, q.buf:q.buf + 1], top[:, q.buf, 0:1], ACT.Copy, scale=-1.0) \
                           .then_inc(nmax_made, 1)
                        act.wait_ge(nmax_made, q.n + 1)
                        act.wait_ge(taken[0], q.n + 1)
                        act.wait_ge(prob_made, past(q.n - NB + 1))
                        act.activation(ex[:, q.buf, :], pS[q.par][:, 0:L], ACT.Exp, bias=nmax[:, q.buf:q.buf + 1]) \
                           .then_inc(exp_made, 1)
                    if o.valid:
                        act.wait_ge(top_found[3], o.n + 1)
                        act.wait_ge(inv_made, past(o.n - NB + 1))
                        act.wait_ge(sum_made, past(o.n))
                        act.activation(extop[:, :], top[:, o.buf, 0:KEEP], ACT.Exp, bias=nmax[:, o.buf:o.buf + 1],
                                       accum_out=rsum[:, o.buf:o.buf + 1]).then_inc(sum_made, 1)
                    if m.valid and m.pair_ends:
                        act.wait_ge(pt_done, m.n + 1)
                        if m.t == 0:
                            act.wait_ge(pv_done, past(m.group - 1))
                        dst, src = PT[m.gpar][0:LC], pT[m.bank][0:LC, :].rearrange("p (t c r) -> p t c r", t=2, c=2)
                        if m.kind == "full":
                            for c in range(2):
                                ins = act.activation(dst[:, m.img, c, m.head - 1:m.head + 1, 0:128], src[:, :, c, :],
                                                     ACT.Copy)
                        elif m.kind == "half":
                            for c in range(2):
                                ins = act.activation(dst[:, m.img, c, m.head - 2:m.head + 2, 128:192],
                                                     src[:, :, c, :].rearrange("p t (h r) -> p t h r", h=2),
                                                     ACT.Copy)
                        else:
                            for i in range(G):
                                v = src[:, 0, :, 64 * i:64 * i + 64].rearrange("p c (h r) -> p c h r", h=H)
                                ins = act.activation(dst[:, i, :, :, 192:L], v[:, :, :, TAILR - (L - 192):TAILR],
                                                     ACT.Copy)
                        ins.then_inc(pt_copied, 1)

                    if t == 5 and s.runs(3):
                        g = s.group(3)
                        act.wait_ge(affT_done, g + 1)
                        act.wait_ge(route_step, past(8 * g))
                        act.activation(affT[:, 0, :], pO[0:G * NX, 0:L], ACT.Copy).then_inc(affT_copied, 1)
                    if t == 7 and s.runs(0):
                        g = s.group(0)
                        act.wait_ge(embedded, g + 1)
                        act.wait_ge(hr_copied, past(16 * g))
                        act.activation(Hs[:, :, :], pA[0:LC, 0:R * D].rearrange("p (r d) -> p r d", r=R), ACT.Copy) \
                           .then_inc(h_copied, 1)
                    if t == 10 and s.runs(0):
                        inv_std(mv, rstd, stat_step, var_exp, newton, s.group(0))
                    if t == 12 and s.runs(0):
                        g = s.group(0)
                        act.wait_ge(newton, 7 * g + 7)
                        act.wait_ge(xnT_done, past(g))
                        for r in range(R):
                            act.activation(xn[:, r, :], Hs[:, r, :], ACT.Identity,
                                           bias=rstd[:, 3, r:r + 1], scale=rstd[:, 2, r:r + 1]).then_inc(xn_made, 1)
                    if t == 12 and s.runs(3):
                        g = s.group(3)
                        act.wait_ge(routeT_done, g + 1)
                        act.wait_ge(slot_done, past(g))
                        act.activation(routeT[:, :, :, :, :],
                                       pD[1][0:CAP, 0:2 * G * NX].rearrange("p (v i c j) -> p v i c j", v=2, i=G, c=NSC),
                                       ACT.Copy).then_inc(routeT_copied, 1)
                    if t == 14 and s.runs(3):
                        g = s.group(3)
                        act.wait_ge(slot_done, g + 1)
                        act.wait_ge(hotS_made, past((G * NSC - HOT_DVE) * g))
                        act.wait_ge(hotS_first, past(HOT_DVE * g))
                        act.activation(slotv[:, :, :, :],
                                       pD[1][0:SC, 0:2 * G * NSC].rearrange("p (v i c) -> p v i c", v=2, i=G),
                                       ACT.Copy).then_inc(slot_copied, 1)
                    if t == 15 and s.runs(0):
                        g = s.group(0)
                        act.wait_ge(xnT_done, g + 1)
                        act.wait_ge(v_done, past(g))
                        act.activation(xnT[:, :, :], pA[:, 0:G * L].rearrange("p (i l) -> p i l", i=G), ACT.Copy) \
                           .then_inc(xnT_copied, 1)
                    if t == 17 and s.runs(0):
                        p, g = s.parity(-1), s.group(0)
                        act.wait_ge(q_done, g + 1)
                        act.wait_ge(q_spread[p], past(16 * H * s.rounds(-1)))
                        act.wait_ge(tail_made, past(g))
                        act.activation(QT[:, :, :], pA[:, 0:G * L].rearrange("p (i l) -> p i l", i=G), ACT.Identity,
                                       bias=bq4[:, 0:1], scale=0.25).then_inc(q_copied, 1)
                    if t == 19 and s.runs(0):
                        p, g = s.parity(0), s.group(0)
                        act.wait_ge(k_done, g + 1)
                        act.activation(KT[p][:, :, :], pA[:, 0:G * L].rearrange("p (i l) -> p i l", i=G), ACT.Identity,
                                       bias=bcol[:, 1:2]).then_inc(k_copied, 1)
                    if t == 21 and s.runs(0):
                        p, g = s.parity(0), s.group(0)
                        act.wait_ge(v_done, g + 1)
                        act.wait_ge(pv_done, past(g - 1))
                        for b in range(2):
                            dst = VP[p][:, :, :, b * E:b * E + E].rearrange("p r (j b) e -> p r j b e", b=2)[:, :, :, b, :]
                            src = pA[0:LC, 0:R * D].rearrange("p (r j b e) -> p r j b e", r=R, b=2, e=E)[:, :, :, b, :]
                            ins = act.activation(dst, src, ACT.Copy)
                        ins.then_inc(v_copied, 1)
                    if t in (18, 20) and s.runs(3):
                        g, i = s.group(3), t // 2 - 9
                        act.wait_ge(xg_done, G * g + i + 1)
                        act.wait_ge(xs_done, past(G * g))
                        act.activation(XG[:, :, i, :], pD[i][:, 0:SLOTS].rearrange("p (e k) -> p e k", e=NX), ACT.Copy) \
                           .then_inc(xg_copied, 1)
                    if t == 11 and s.runs(2):
                        g = s.group(2)
                        act.wait_ge(pv_done, g + 1)
                        act.wait_ge(proj_done, past(g))
                        act.activation(OT[:, :, :], pO[:, 0:G * L].rearrange("p (i l) -> p i l", i=G), ACT.Identity,
                                       bias=bcol[:, 2:3]).then_inc(o_copied, 1)
                    if 15 <= t < 19 and s.runs(3):
                        i, c = divmod(t - 15, 2)
                        g, n = s.group(3), 2 * i + c
                        act.wait_ge(bc_done, G * g + i + 1)
                        act.wait_ge(y_done, past(g))
                        act.activation(hotG[:, n, :], pD[i][0:LC, 0:SLOTS], ACT.Abs, bias=minus_tok[:, c:c + 1]) \
                           .then_inc(far_made, 1)
                        act.wait_ge(far_made, R * g + n + 1)
                        act.activation(hotG[:, n, :], hotG[:, n, :], ACT.Relu, bias=one_col[:, 0:1], scale=-1.0) \
                           .then_inc(hotG_made, 1)
                    if t == 14 and s.runs(2):
                        p, g = s.parity(2), s.group(2)
                        act.wait_ge(proj_done, g + 1)
                        act.wait_ge(y_done, past(g - 1))
                        act.activation(H1[p][:, :, :], pO[0:LC, 0:R * D].rearrange("p (r d) -> p r d", r=R), ACT.Copy) \
                           .then_inc(h1_copied, 1)
                    if t == 0 and s.runs(4):
                        g = s.group(4)
                        for a in range(2):
                            act.wait_ge(m1_done, 2 * g + a + 1)
                            act.wait_ge(m2_done, past(2 * g))
                            act.activation(HID[:, NX // 2 * a:NX // 2 * (a + 1), :],
                                           pD[a][:, 0:SLOTS].rearrange("p (e k) -> p e k", e=NX // 2),
                                           ACT.Gelu_apprx_tanh).then_inc(gelu_made, 1)
                        act.preload_act_table_set(EXP_LN_TABLES)
                    if t == 17 and s.runs(2):
                        inv_std(mv2, rstd2, stat2_step, var2_exp, newton2, s.group(2))
                    if t in (5, 7) and s.runs(4):
                        g, a = s.group(4), t // 2 - 2
                        act.wait_ge(m2_done, 2 * g + a + 1)
                        act.wait_ge(xs_done, past(G * g))
                        act.activation(XE[:, :, NX // 2 * a:NX // 2 * (a + 1), :].rearrange("p i e k -> p e i k"),
                                       pD[a][:, 0:SLOTS].rearrange("p (e i k) -> p e i k", e=NX // 2, i=G),
                                       ACT.Copy).then_inc(xe_copied, 1)
                    if t == 20 and s.runs(2):
                        p, g = s.parity(2), s.group(2)
                        act.wait_ge(newton2, 7 * g + 7)
                        act.wait_ge(xg_done, past(G * (g - 1)))
                        for r in range(R):
                            act.activation(xn2[p][:, r, :], H1[p][:, r, :], ACT.Identity,
                                           bias=rstd2[:, 3, r:r + 1], scale=rstd2[:, 2, r:r + 1]).then_inc(xn2_made, 1)
                    if t == 8 and s.runs(4):
                        g = s.group(4)
                        for i in range(G):
                            act.wait_ge(xs_done, G * g + i + 1)
                            act.wait_ge(y_done, past(g))
                            act.activation(XS[:, i, :, :], pD[i][0:SC, 0:NSC * D].rearrange("p (c d) -> p c d", c=NSC),
                                           ACT.Copy).then_inc(xs_copied, 1)
                    if t == 23 and s.runs(2):
                        g = s.group(2)
                        act.wait_ge(xn2T_done, g + 1)
                        act.wait_ge(logit_done, past(g))
                        act.activation(xn2T[:, :, :], pA[:, 0:G * L].rearrange("p (i l) -> p i l", i=G), ACT.Copy) \
                           .then_inc(xn2T_copied, 1)
                    if t == 2 and s.runs(3):
                        g = s.group(3)
                        act.wait_ge(lsh_made, g + 1)
                        act.wait_ge(aff_made, past(g))
                        act.activation(lex[:, :, :], lsh[:, :, :], ACT.Exp).then_inc(lex_made, 1)
                    if t == 13 and s.runs(4):
                        g = s.group(4)
                        act.wait_ge(y_done, g + 1)
                        act.wait_ge(stored, past(16 * g))
                        act.activation(Y[:, :, :], pD[0][0:LC, 0:R * D].rearrange("p (r d) -> p r d", r=R), ACT.Copy) \
                           .then_inc(y_copied, 1)

            all_steps(body, act)

        @block.tensor
        def _(pe):
            pe.wait_ge(w_raw, 16 * 5)
            pe.wait_ge(ident_ready, 1)
            pe.wait_ge(wsorted, 1)
            for n in range(QS + 4):
                pe.wait_ge(wt_copied, past(n - 1))
                if n < QS:
                    cols = min(SH, P - SH * n)
                    src = wsort[:, SH * n * CP:(SH * n + cols) * CP]
                    pe.transpose(pT[n % 2][0:cols * CP, 0:D], src, ident[:, :]).then_inc(wt_done, 1)
                else:
                    pe.transpose(pT[n % 2][:, 0:D], wraw[:, n - QS, :], ident[:, :]).then_inc(wt_done, 1)
            pe.wait_ge(wt_copied, QS + 4)
            pe.wait_ge(w_loaded, 16 * N_W_LOADS)
            pe.wait_ge(posb_ready, 1)
            pe.wait_ge(bias_split, 7)
            pe.wait_ge(exp_sel_step, 3)
            pe.wait_ge(const_step, 4 + G)
            pe.wait_ge(zero_ready, 4)

            def chunk(i, c):
                return slice(i * L + c * LC, i * L + (c + 1) * LC)

            def score(q, par):
                pe.wait_ge(exp_made, past(q.n - 1))
                if q.t == 0:
                    pe.wait_ge(k_copied, q.group + 1)
                qm, k = QM[q.gpar], KT[q.gpar]
                dst = pS[q.par]
                if q.kind == "full":
                    pe.matmul(dst[:, 0:L], qm[:, q.img, q.head, 0:128], k[:, q.img, :], start=True, stop=True) \
                      .then_inc(scored, 1)
                elif q.kind == "half":
                    for b in range(2):
                        ins = pe.matmul(dst[64 * b:64 * b + 64, 0:L], qm[:, q.img, q.head + b, 128:192],
                                        k[:, q.img, :], start=True, stop=True)
                    ins.then_inc(scored, 1)
                else:
                    for i in range(G):
                        ins = pe.matmul(dst[64 * i:64 * i + 64, 0:L], QMtail[q.gpar][:, i, :], k[:, i, :],
                                        start=True, stop=True)
                    ins.then_inc(scored, 1)

            def experts(layer, a, part, src, done):
                w = (w1s, w2s)[layer]
                if part == 0:
                    pe.matmul(pD[a][:, 0:SLOTS], bias3[:, layer, :],
                              exp_sel[:, NX // 2 * a:NX // 2 * (a + 1)].rearrange("p (e k) -> p e k", k=1)
                              .broadcast_to([96, NX // 2, G * CAP]),
                              start=True, stop=False)
                for n in range(NX // 4 * part, NX // 4 * (part + 1)):
                    e = NX // 2 * a + n
                    rhs = src[:, e, :, :].rearrange("p i k -> p (i k)") if layer == 0 else src[:, e, :]
                    ins = pe.matmul(pD[a][:, G * CAP * n:G * CAP * (n + 1)], w[:, e, :], rhs,
                                    start=False, stop=n == NX // 2 - 1)
                if part == 1:
                    ins.then_inc(done, 1)

            def body(s):
                for t in range(T):
                    q, m = s.tile(t), s.tile(t - PE_LAG)
                    if q.valid:
                        if t == 0:
                            pe.wait_ge(q_spread[q.gpar], 16 * H * (s.rounds(1) + 1))
                            pe.wait_ge(tail_made, s.group(1) + 1)
                        score(q, s.par)

                    if t < len(EMBED) and s.runs(0):
                        g = s.group(0)
                        if t == 0:
                            pe.wait_ge(x_loaded, 16 * G * SH * C * (g + 1))
                            pe.wait_ge(v_copied, past(g))
                            pe.wait_ge(xn2T_copied, past(g - 2))
                        for n in range(sum(EMBED[:t]), sum(EMBED[:t + 1])):
                            r, part = divmod(n, QS + 1)
                            i, c = divmod(r, 2)
                            dst = pA[0:LC, r * D:r * D + D]
                            if part < QS:
                                kp = min(SH, P - SH * part) * CP
                                lo = XPAD + P * (LC * c - 2) + SH * part
                                src = X[0:kp, i, lo:lo + P * (LC - 1) + 1:P]
                                ins = pe.matmul(dst, src, tokWT[0:kp, part, :], start=part == 0, stop=False)
                            else:
                                ins = pe.matmul(dst, ident[0:LC, 0:LC], posb[:, c, :], start=False, stop=True)
                        if t == len(EMBED) - 1:
                            ins.then_inc(embedded, 1)
                    if t == 16 and s.runs(0):
                        g = s.group(0)
                        pe.wait_ge(xn_made, R * g + R)
                        for r in range(R):
                            ins = pe.transpose(pA[:, chunk(r // 2, r % 2)], xn[:, r, :], ident[0:LC, 0:LC])
                        ins.then_inc(xnT_done, 1)
                    if t == 18 and s.runs(0):
                        pe.wait_ge(xnT_copied, s.group(0) + 1)
                        pe.matmul(pA[:, 0:G * L], WT[:, 0, :], xnT[:, :, :], start=True, stop=True).then_inc(q_done, 1)
                    if t == 20 and s.runs(0):
                        pe.wait_ge(q_copied, s.group(0) + 1)
                        pe.matmul(pA[:, 0:G * L], WT[:, 1, :], xnT[:, :, :], start=True, stop=True).then_inc(k_done, 1)
                    if t == 22 and s.runs(0):
                        pe.wait_ge(k_copied, s.group(0) + 1)
                        for r in range(R):
                            ins = pe.matmul(pA[0:LC, r * D:r * D + D], xnT[:, r // 2, LC * (r % 2):LC * (r % 2 + 1)],
                                            WT[:, 2, :], start=True, stop=True)
                        ins.then_inc(v_done, 1)

                    if 8 <= t < 12 and s.runs(2):
                        p, g = s.parity(2), s.group(2)
                        if t == 8:
                            pe.wait_ge(affT_copied, past(g))
                            pe.wait_ge(pt_copied, (g + 1) * PAIRS)
                            pe.wait_ge(v_copied, g + 1)
                        i, b = divmod(t - 8, 2)
                        for c, j in ((c, j) for c in range(2) for j in range(4)):
                            h = 2 * j + b
                            ins = pe.matmul(pO[32 * j:32 * j + 32, i * L:i * L + L], VP[p][:, 2 * i + c, h, :],
                                            PT[p][0:LC, i, c, h, :], start=b + c == 0, stop=b + c == 2)
                        if t == 11:
                            ins.then_inc(pv_done, 1)
                    if t in (14, 15) and s.runs(2):
                        p, g = s.parity(2), s.group(2)
                        if t == 14:
                            pe.wait_ge(o_copied, g + 1)
                            pe.wait_ge(hr_copied, 16 * (g + 1))
                            pe.matmul(pO[0:LC, 0:R * D], ones3[:, :], bias3[:, 2:3, :].broadcast_to([96, R, D]),
                                      start=True, stop=False)
                        for r in range(2 * (t - 14), 2 * (t - 14) + 2):
                            dst = pO[0:LC, r * D:r * D + D]
                            pe.matmul(dst, OT[:, r // 2, LC * (r % 2):LC * (r % 2 + 1)], WT[:, 3, :],
                                      start=False, stop=False)
                            ins = pe.matmul(dst, ident[0:LC, 0:LC], HR[p][:, r, :], start=False, stop=r == R - 1)
                        if t == 15:
                            ins.then_inc(proj_done, 1)
                    if t == 24 and s.runs(2):
                        g = s.group(2)
                        pe.wait_ge(xn2_made, R * g + R)
                        if s.runs(0):
                            pe.wait_ge(v_copied, s.group(0) + 1)
                        for r in range(R):
                            ins = pe.transpose(pA[:, chunk(r // 2, r % 2)], xn2[s.parity(2)][:, r, :],
                                               ident[0:LC, 0:LC])
                        ins.then_inc(xn2T_done, 1)
                    if t == 1 and s.runs(3):
                        g = s.group(3)
                        if s.known():
                            pe.wait_ge(experts_loaded, 16 * 3)
                        pe.wait_ge(h1_copied, g + 1)
                        pe.wait_ge(xn2T_copied, g + 1)
                        for r in range(R):
                            ins = pe.matmul(pO[0:LC, r * NX:r * NX + NX],
                                            xn2T[:, r // 2, LC * (r % 2):LC * (r % 2 + 1)], gw[:, :],
                                            start=True, stop=True)
                        ins.then_inc(logit_done, 1)

                    if t == 6 and s.runs(3):
                        g = s.group(3)
                        pe.wait_ge(aff_made, g + 1)
                        pe.wait_ge(lsh_made, g + 1)
                        for c in range(2):
                            ins = pe.transpose(pO[0:G * NX, LC * c:LC * c + LC],
                                               aff[:, c, :, :].rearrange("p i e -> p (i e)"), ident[0:LC, 0:LC])
                        ins.then_inc(affT_done, 1)
                    if t == 13 and s.runs(3):
                        g = s.group(3)
                        settle(pe, g + 1, G * g)
                        pe.wait_ge(routed, g + 1)
                        pe.wait_ge(xs_copied, past(G * g))
                        for v in range(2):
                            ins = pe.transpose(pD[1][0:CAP, G * NX * v:G * NX * (v + 1)], route[:, v, :],
                                               ident[0:G * NX, 0:G * NX])
                        ins.then_inc(routeT_done, 1)
                    if t == 15 and s.runs(3):
                        g = s.group(3)
                        pe.wait_ge(routeT_copied, g + 1)
                        for j in range(EPC):
                            ins = pe.matmul(pD[1][0:SC, 0:2 * G * NSC], slot_sel[:, j, :],
                                            routeT[:, :, :, :, j].rearrange("p v i c -> p (v i c)"),
                                            start=j == 0, stop=j == EPC - 1)
                        ins.then_inc(slot_done, 1)
                    if t in (16, 17) and s.runs(3):
                        g, i = s.group(3), t - 16
                        if i == 0:
                            pe.wait_ge(spread_made, g + 1)
                            pe.wait_ge(y_copied, past(g))
                        else:
                            pe.wait_ge(slot_copied, g + 1)
                        pe.matmul(pD[i][0:LC, 0:SLOTS], img_sel[:, i, :],
                                  spread[:, :, :].rearrange("p e k -> p (e k)"),
                                  start=True, stop=True).then_inc(bc_done, 1)
                    if 18 <= t < 22 and s.runs(3):
                        g, i, c = s.group(3), (t - 18) // 2, t % 2
                        pe.wait_ge(hotG_made, R * g + 2 * i + c + 1)
                        if c == 0:
                            pe.wait_ge(hotG_made, R * g + 2 * i + 2)
                        ins = pe.matmul(pD[i][:, 0:SLOTS], xn2[s.parity(3)][:, 2 * i + c, :], hotG[:, 2 * i + c, :],
                                        start=c == 0, stop=c == 1)
                        if c == 1:
                            ins.then_inc(xg_done, 1)
                    late = t < 2
                    if (late and s.runs(4)) or (t >= 23 and s.runs(3)):
                        g, a, part = s.group(4 if late else 3), int(late), (t + 1) % 2 if not late else t
                        if not late and part == 0:
                            pe.wait_ge(xg_copied, G * (g + 1))
                        experts(0, a, part, XG, m1_done)
                    if 4 <= t < 8 and s.runs(4):
                        g, a, part = s.group(4), t // 2 - 2, t % 2
                        pe.wait_ge(gelu_made, 2 * g + a + 1)
                        experts(1, a, part, HID, m2_done)
                    if t == 9 and s.runs(4):
                        g = s.group(4)
                        pe.wait_ge(xe_copied, 2 * (g + 1))
                        for i in range(G):
                            for c in range(NSC):
                                ins = pe.transpose(pD[i][0:SC, D * c:D * c + D],
                                                   XE[:, i, EPC * c:EPC * (c + 1), :].rearrange("p e k -> p (e k)"),
                                                   ident[:, :])
                            ins.then_inc(xs_done, 1)
                    if t in (11, 12, 13, 14) and s.runs(4):
                        g, r = s.group(4), t - 11
                        i, c = divmod(r, 2)
                        pe.wait_ge(xs_copied, G * g + G)
                        pe.wait_ge(hotS_made, (G * NSC - HOT_DVE) * (g + 1))
                        pe.wait_ge(hotS_first, HOT_DVE * (g + 1))
                        dst = pD[0][0:LC, r * D:r * D + D]
                        pe.matmul(dst, ident[0:LC, 0:LC], H1[s.parity(4)][:, r, :], start=True, stop=False)
                        for n in range(NSC):
                            ins = pe.matmul(dst, hotS[:, i, n, LC * c:LC * c + LC], XS[:, i, n, :],
                                            start=False, stop=n == NSC - 1)
                        if r == R - 1:
                            ins.then_inc(y_done, 1)

                    if m.valid:
                        pe.wait_ge(prob_made, m.n + 1)
                        if m.pair_starts:
                            pe.wait_ge(pt_copied, past(m.pairs - 1))
                        for c in range(2):
                            at = 256 * m.side + 128 * c
                            ins = pe.transpose(pT[m.bank][0:LC, at:at + 128], prob[:, m.buf, LC * c:LC * c + LC],
                                               ident[:, :])
                        ins.then_inc(pt_done, 1)

            all_steps(body, pe)


_INS = ['x', 'cls_tok', 'L0_tok_W', 'L0_tok_b', 'L0_tok_token', 'L0_tok_pos', 'L0_attn_Wq', 'L0_attn_bq',
        'L0_attn_Wk', 'L0_attn_bk', 'L0_attn_Wv', 'L0_attn_bv', 'L0_attn_Wo', 'L0_attn_bo',
        'L0_ffn_gate_weight', 'L0_ffn_w1', 'L0_ffn_b1', 'L0_ffn_w2', 'L0_ffn_b2']
_OUT = (64, 198, 128)


def kernel(**inputs):
    import numpy as _np
    import concourse.bacc as _bacc
    from concourse import mybir as _mybir
    from concourse.bass_utils import run_bass_kernel_spmd as _run

    nc = _bacc.Bacc("TRN2", target_bir_lowering=False, num_devices=1)
    arrays, args = {}, []
    for name in _INS:
        a = _np.ascontiguousarray(inputs[name])
        arrays[f"in_{name}_dram"] = a
        args.append(nc.dram_tensor(f"in_{name}_dram", a.shape, _mybir.dt.from_np(a.dtype), kind="ExternalInput").ap())
    out = nc.dram_tensor("out_dram", _OUT, _mybir.dt.float32, kind="ExternalOutput").ap()
    vit_block(nc, *args, out)
    r = _run(nc, [arrays], core_ids=[0])
    return r.results[0]["out_dram"]
```
